# Optimizing a Trainium2 kernel written in Bass

```python
import numpy as np
import jax
import jax.numpy as jnp

def _softmax(x, axis=-1):
    return jax.nn.softmax(x, axis=axis)

def _gelu(x):
    return jax.nn.gelu(x, approximate=True)

def _silu(x):
    return jax.nn.silu(x)

def _sigmoid(x):
    return jax.nn.sigmoid(x)

def _layernorm(x, axis=-1, eps=1e-05):
    m = jnp.mean(x, axis=axis, keepdims=True)
    v = jnp.var(x, axis=axis, keepdims=True)
    return (x - m) / jnp.sqrt(v + eps)

def _scatter_add(tgt, idx, src, axis=0):
    return tgt.at[idx].add(src)

def _segment_sum(src, seg, n):
    return jax.ops.segment_sum(src, seg, n)
kernel_name = 'mk_cond_seq_d2_seqx_r2_c2df9b'

def setup_inputs(seed: int=0):
    np.random.seed(seed)
    _w = jnp.asarray

    def _rec_inputs():
        import jax
        import jax.numpy as jnp
        _rk = jax.random.key(seed)
        x = -0.000125 + 0.9999 * jax.random.normal(jax.random.fold_in(_rk, 1), (4, 1024, 512), jnp.float32)
        _lenS = 1024 - jax.random.randint(jax.random.fold_in(_rk, 7), (4,), 0, max(1, 1024 // 4) + 1, jnp.int32)
        _lenS2 = 1024 - jax.random.randint(jax.random.fold_in(_rk, 8), (4,), 0, max(1, 1024 // 4) + 1, jnp.int32)
        condB_safetyscore = -0.927215 + 0.920279 * jax.random.normal(jax.random.fold_in(_rk, 11), (4,), jnp.float32)
        itok_B_34_63 = jax.random.randint(jax.random.fold_in(_rk, 13), (4,), 34, 64, jnp.int32)
        fside_Bx16xSxS_0 = -1.47943e-05 + 1.00017 * jax.random.normal(jax.random.fold_in(_rk, 14), (4, 16, 1024, 1024), jnp.float32)
        _validS = jnp.arange(1024)[None, :] < _lenS[:, None]
        _validS2 = jnp.arange(1024)[None, :] < _lenS2[:, None]
        _causal = jnp.tril(jnp.ones((1024, 1024), dtype=bool))
        mask_Bx1xSxS_bk0 = jnp.logical_not(jnp.broadcast_to(_validS[:, None, None, :], (4, 1, 1024, 1024)))
        return (x, condB_safetyscore, itok_B_34_63, fside_Bx16xSxS_0, mask_Bx1xSxS_bk0)
    x, condB_safetyscore, itok_B_34_63, fside_Bx16xSxS_0, mask_Bx1xSxS_bk0 = _rec_inputs()

    def _L0_cond_setup():
        import jax, jax.numpy as jnp
        import numpy as np
        TEMPERATURE = 1.0
        ACT_THRESHOLD = 0.1
        MAX_ACT = 1.0
        SAFETY_KNOB = 1.0
        EPS = 1e-08

        def gram_schmidt(X):
            r = X.shape[1]
            Q = X
            for i in range(r):
                q = Q[:, i]
                q = q / (jnp.linalg.norm(q) + EPS)
                Q = Q.at[:, i].set(q)
                coeffs = q @ Q[:, i + 1:]
                Q = Q.at[:, i + 1:].add(-jnp.outer(q, coeffs))
            return Q
        key = jax.random.key(seed)
        ks = jax.random.split(key, 8)
        B, S, D, R = (8, 2048, 512, 32)
        init_std = 0.02
        return {'hidden_states': jax.random.normal(ks[0], (B, S, D), jnp.float32), 'safety_score': jax.random.normal(ks[1], (B,), jnp.float32), 'U': jax.random.normal(ks[2], (D, R), jnp.float32) * init_std, 'V': jax.random.normal(ks[3], (D, R), jnp.float32) * init_std, 'safety_bias': jnp.zeros((D,), jnp.float32), 'gate_w1': jax.random.normal(ks[4], (D // 4, D), jnp.float32) * (1.0 / np.sqrt(D)), 'gate_b1': jnp.zeros((D // 4,), jnp.float32), 'gate_w2': jax.random.normal(ks[5], (1, D // 4), jnp.float32) * (1.0 / np.sqrt(D // 4)), 'gate_b2': jnp.zeros((1,), jnp.float32), 'resp_w': jax.random.normal(ks[6], (D, R), jnp.float32) * (1.0 / np.sqrt(R)), 'resp_b': jnp.zeros((D,), jnp.float32)}
    _L0_cond_all = _L0_cond_setup()
    _L0_cond_in = {k: v for k, v in _L0_cond_all.items() if k in ('U', 'V', 'safety_bias', 'gate_w1', 'gate_b1', 'gate_w2', 'gate_b2', 'resp_w', 'resp_b')}
    del _L0_cond_all

    def _L1_cond_setup():
        import jax, jax.numpy as jnp
        import numpy as np
        import math
        D_MODEL = 512
        N_HEAD = 16
        HEAD_DIM = D_MODEL // N_HEAD
        D_FF = 2048
        NUM_STEPS = 100.0
        RESCALE = 4000.0
        EPS = 1e-05

        def _sin_emb(t):
            half = D_MODEL // 2
            x = t.astype(jnp.float32) / NUM_STEPS * RESCALE
            freqs = jnp.exp(jnp.arange(half, dtype=jnp.float32) * (-math.log(10000.0) / (half - 1)))
            e = x[:, None] * freqs[None, :]
            return jnp.concatenate([jnp.sin(e), jnp.cos(e)], axis=-1)

        def _ln(x):
            m = jnp.mean(x, axis=-1, keepdims=True)
            v = jnp.var(x, axis=-1, keepdims=True)
            return (x - m) / jnp.sqrt(v + EPS)

        def _gelu2(x):
            return x * jax.nn.sigmoid(1.702 * x)
        key = jax.random.key(seed)
        ks = jax.random.split(key, 24)
        B, S, D, F = (4, 256, D_MODEL, D_FF)
        std = 0.02
        inp = {'src': jax.random.normal(ks[0], (B, S, D), dtype=jnp.float32), 'src_mask': jax.random.randint(ks[1], (B, 1, S, S), 0, 2).astype(bool), 'timestep': jax.random.randint(ks[2], (B,), 0, 100, dtype=jnp.int32), 'attention_bias': jax.random.normal(ks[3], (B, N_HEAD, S, S), dtype=jnp.float32), 'W_ada': jax.random.normal(ks[4], (D, 2 * D), dtype=jnp.float32) * std, 'b_ada': jnp.zeros((2 * D,), dtype=jnp.float32), 'Wq': jax.random.normal(ks[5], (D, D), dtype=jnp.float32) * std, 'bq': jnp.zeros((D,), dtype=jnp.float32), 'Wk': jax.random.normal(ks[6], (D, D), dtype=jnp.float32) * std, 'bk': jnp.zeros((D,), dtype=jnp.float32), 'Wv': jax.random.normal(ks[7], (D, D), dtype=jnp.float32) * std, 'bv': jnp.zeros((D,), dtype=jnp.float32), 'Wo': jax.random.normal(ks[8], (D, D), dtype=jnp.float32) * std, 'bo': jnp.zeros((D,), dtype=jnp.float32), 'W1': jax.random.normal(ks[9], (D, F), dtype=jnp.float32) * std, 'b1': jnp.zeros((F,), dtype=jnp.float32), 'W2': jax.random.normal(ks[10], (F, D), dtype=jnp.float32) * std, 'b2': jnp.zeros((D,), dtype=jnp.float32), 'g2': jnp.ones((D,), dtype=jnp.float32), 'beta2': jnp.zeros((D,), dtype=jnp.float32)}
        return inp
    _L1_cond_all = _L1_cond_setup()
    _L1_cond_in = {k: v for k, v in _L1_cond_all.items() if k in ('W_ada', 'b_ada', 'Wq', 'bq', 'Wk', 'bk', 'Wv', 'bv', 'Wo', 'bo', 'W1', 'b1', 'W2', 'b2', 'g2', 'beta2')}
    del _L1_cond_all
    return {'x': x, 'condB_safetyscore': condB_safetyscore, 'itok_B_34_63': itok_B_34_63, 'fside_Bx16xSxS_0': fside_Bx16xSxS_0, 'mask_Bx1xSxS_bk0': mask_Bx1xSxS_bk0, 'L0_cond_U': _L0_cond_in['U'], 'L0_cond_V': _L0_cond_in['V'], 'L0_cond_safety_bias': _L0_cond_in['safety_bias'], 'L0_cond_gate_w1': _L0_cond_in['gate_w1'], 'L0_cond_gate_b1': _L0_cond_in['gate_b1'], 'L0_cond_gate_w2': _L0_cond_in['gate_w2'], 'L0_cond_gate_b2': _L0_cond_in['gate_b2'], 'L0_cond_resp_w': _L0_cond_in['resp_w'], 'L0_cond_resp_b': _L0_cond_in['resp_b'], 'L1_cond_W_ada': _L1_cond_in['W_ada'], 'L1_cond_b_ada': _L1_cond_in['b_ada'], 'L1_cond_Wq': _L1_cond_in['Wq'], 'L1_cond_bq': _L1_cond_in['bq'], 'L1_cond_Wk': _L1_cond_in['Wk'], 'L1_cond_bk': _L1_cond_in['bk'], 'L1_cond_Wv': _L1_cond_in['Wv'], 'L1_cond_bv': _L1_cond_in['bv'], 'L1_cond_Wo': _L1_cond_in['Wo'], 'L1_cond_bo': _L1_cond_in['bo'], 'L1_cond_W1': _L1_cond_in['W1'], 'L1_cond_b1': _L1_cond_in['b1'], 'L1_cond_W2': _L1_cond_in['W2'], 'L1_cond_b2': _L1_cond_in['b2'], 'L1_cond_g2': _L1_cond_in['g2'], 'L1_cond_beta2': _L1_cond_in['beta2']}

def reference(x, condB_safetyscore, itok_B_34_63, fside_Bx16xSxS_0, mask_Bx1xSxS_bk0, L0_cond_U, L0_cond_V, L0_cond_safety_bias, L0_cond_gate_w1, L0_cond_gate_b1, L0_cond_gate_w2, L0_cond_gate_b2, L0_cond_resp_w, L0_cond_resp_b, L1_cond_W_ada, L1_cond_b_ada, L1_cond_Wq, L1_cond_bq, L1_cond_Wk, L1_cond_bk, L1_cond_Wv, L1_cond_bv, L1_cond_Wo, L1_cond_bo, L1_cond_W1, L1_cond_b1, L1_cond_W2, L1_cond_b2, L1_cond_g2, L1_cond_beta2):
    import jax
    import jax.numpy as jnp

    def _L0_cond_ref(hidden_states, safety_score, U, V, safety_bias, gate_w1, gate_b1, gate_w2, gate_b2, resp_w, resp_b):
        import jax, jax.numpy as jnp
        import numpy as np
        TEMPERATURE = 1.0
        ACT_THRESHOLD = 0.1
        MAX_ACT = 1.0
        SAFETY_KNOB = 1.0
        EPS = 1e-08

        def gram_schmidt(X):
            r = X.shape[1]
            Q = X
            for i in range(r):
                q = Q[:, i]
                q = q / (jnp.linalg.norm(q) + EPS)
                Q = Q.at[:, i].set(q)
                coeffs = q @ Q[:, i + 1:]
                Q = Q.at[:, i + 1:].add(-jnp.outer(q, coeffs))
            return Q
        R = resp_w.shape[1]
        U_o = gram_schmidt(U)
        V_o = gram_schmidt(V)
        basis = U_o @ V_o.T
        pooled = hidden_states.mean(axis=1)
        h1 = jax.nn.relu(pooled @ gate_w1.T + gate_b1)
        base_act = jax.nn.sigmoid(h1 @ gate_w2.T + gate_b2)
        mod = jax.nn.sigmoid(safety_score[:, None] / TEMPERATURE)
        knob = jnp.clip(jnp.asarray(SAFETY_KNOB, hidden_states.dtype), ACT_THRESHOLD, MAX_ACT)
        strength = (base_act * mod * knob)[:, None, :]
        proj = hidden_states @ basis
        feats = proj @ basis.T[:, :R]
        response = feats @ resp_w.T + resp_b + safety_bias
        return hidden_states + strength * response

    def _L1_cond_ref(src, src_mask, timestep, attention_bias, W_ada, b_ada, Wq, bq, Wk, bk, Wv, bv, Wo, bo, W1, b1, W2, b2, g2, beta2):
        import jax, jax.numpy as jnp
        import numpy as np
        import math
        D_MODEL = 512
        N_HEAD = 16
        HEAD_DIM = D_MODEL // N_HEAD
        D_FF = 2048
        NUM_STEPS = 100.0
        RESCALE = 4000.0
        EPS = 1e-05

        def _sin_emb(t):
            half = D_MODEL // 2
            x = t.astype(jnp.float32) / NUM_STEPS * RESCALE
            freqs = jnp.exp(jnp.arange(half, dtype=jnp.float32) * (-math.log(10000.0) / (half - 1)))
            e = x[:, None] * freqs[None, :]
            return jnp.concatenate([jnp.sin(e), jnp.cos(e)], axis=-1)

        def _ln(x):
            m = jnp.mean(x, axis=-1, keepdims=True)
            v = jnp.var(x, axis=-1, keepdims=True)
            return (x - m) / jnp.sqrt(v + EPS)

        def _gelu2(x):
            return x * jax.nn.sigmoid(1.702 * x)
        B, S, D = src.shape
        emb = jax.nn.silu(_sin_emb(timestep)) @ W_ada + b_ada
        scale, shift = jnp.split(emb[:, None, :], 2, axis=-1)
        x = _ln(src) * (1.0 + scale) + shift
        q = (x @ Wq + bq).reshape(B, S, N_HEAD, HEAD_DIM).transpose(0, 2, 1, 3)
        k = (x @ Wk + bk).reshape(B, S, N_HEAD, HEAD_DIM).transpose(0, 2, 1, 3)
        v = (x @ Wv + bv).reshape(B, S, N_HEAD, HEAD_DIM).transpose(0, 2, 1, 3)
        scores = jnp.einsum('bhqd,bhkd->bhqk', q / math.sqrt(HEAD_DIM), k)
        scores = scores + attention_bias
        scores = jnp.where(src_mask, -jnp.inf, scores.astype(jnp.float32))
        probs = jax.nn.softmax(scores, axis=-1).astype(v.dtype)
        ctx = jnp.einsum('bhqk,bhkd->bhqd', probs, v)
        ctx = ctx.transpose(0, 2, 1, 3).reshape(B, S, D)
        x = x + (ctx @ Wo + bo)
        h = _ln(x) * g2 + beta2
        ff = _gelu2(h @ W1 + b1) @ W2 + b2
        return x + ff
    x = _L0_cond_ref(x, condB_safetyscore, L0_cond_U, L0_cond_V, L0_cond_safety_bias, L0_cond_gate_w1, L0_cond_gate_b1, L0_cond_gate_w2, L0_cond_gate_b2, L0_cond_resp_w, L0_cond_resp_b)
    x = _L1_cond_ref(x, mask_Bx1xSxS_bk0, itok_B_34_63, fside_Bx16xSxS_0, L1_cond_W_ada, L1_cond_b_ada, L1_cond_Wq, L1_cond_bq, L1_cond_Wk, L1_cond_bk, L1_cond_Wv, L1_cond_bv, L1_cond_Wo, L1_cond_bo, L1_cond_W1, L1_cond_b1, L1_cond_W2, L1_cond_b2, L1_cond_g2, L1_cond_beta2)
    return x

_drawn_inputs = setup_inputs


def setup_inputs(seed=0):
    import zlib

    import numpy as np

    out = dict(_drawn_inputs(seed))
    spreads = {'L0_cond_safety_bias': (0.0, 0.462),
     'L0_cond_gate_b1': (0.0, 0.8),
     'L0_cond_resp_b': (0.0, 0.424),
     'L1_cond_b_ada': (0.0, 0.1),
     'L1_cond_bq': (0.0, 0.8),
     'L1_cond_bk': (0.0, 0.8),
     'L1_cond_bv': (0.0, 0.1),
     'L1_cond_bo': (0.0, 0.1),
     'L1_cond_b1': (0.0, 0.1),
     'L1_cond_b2': (0.0, 0.1),
     'L1_cond_g2': (1.0, 0.2),
     'L1_cond_beta2': (0.0, 0.335)}
    factors = {'condB_safetyscore': 2.926,
     'fside_Bx16xSxS_0': 6.36,
     'L0_cond_V': 8.0,
     'L0_cond_gate_w1': 8.0,
     'L0_cond_gate_w2': 8.0,
     'L1_cond_Wq': 8.0,
     'L1_cond_Wk': 8.0}
    for name, (base, spread) in spreads.items():
        noise = np.random.default_rng([zlib.crc32(name.encode()), seed]).standard_normal(out[name].shape)
        drawn = base * np.exp(spread * noise) if base else spread * noise
        out[name] = jnp.asarray(drawn.astype(out[name].dtype))
    for name, factor in factors.items():
        out[name] = (out[name] * factor).astype(out[name].dtype)
    return out
```

```python
import math
from contextlib import ExitStack

import numpy as np

import concourse.bass as bass
from concourse import mybir

F32 = mybir.dt.float32
F32R = mybir.dt.float32r
BF16 = mybir.dt.bfloat16
I32 = mybir.dt.int32
U8 = mybir.dt.uint8
ALU = mybir.AluOpType
ACT = mybir.ActivationFunctionType

P = 128
B, S, D, H = 4, 1024, 512, 16
HD = D // H
R = 32
FF = 2048
KC = D // P
FC = FF // P
TB = 512
NT = TB // P
NBLK = B * S // TB
HG = 4
NG = B * H // HG
NQT = S // P
NKC = S // P
QP = 2 * P
NQP = S // QP
UQ = HG * QP // P
UG = NQP * UQ
NBIAS = 8
POOL_HEADS = (0, 1, 2)
MASKED = -1.0e30
HUGE = 3.0e38
LN_EPS = 1e-5
CW = 3 * D + 4
RING = 4

ROUND = 12582912.0
TWO_PI = (6.28125, 0.0019340515136718750, float(2 * math.pi - 6.28125 - 0.0019340515136718750))
PI_MAX = 3.1415925


def at_least(eng, sem, value):
    if isinstance(value, int) and value <= 0:
        return
    eng.wait_ge(sem, value)


def carried(eng, sem):
    eng.wait_ge(sem, 1)


def counted(eng, value):
    return value if isinstance(value, int) else eng.to_reg(value)


def chain_on(eng, sem):
    count = [0]

    def link(ins):
        count[0] += 1
        ins.then_inc(sem, 1)
        eng.wait_ge(sem, count[0])
        return ins

    return link


class Scope:

    def __init__(self, nc, ctx, prefix):
        self.nc, self.ctx, self.prefix, self.taken = nc, ctx, prefix, []

    def sb(self, name, shape, dt=F32):
        return self.ctx.enter_context(self.nc.sbuf_tensor(self.prefix + name, shape, dt))

    def ps(self, name, shape):
        return self.ctx.enter_context(self.nc.psum_tensor(self.prefix + name, shape, F32))

    def sem(self, name):
        self.taken.append(self.nc.alloc_semaphore(self.prefix + name))
        return self.taken[-1]

    def sems(self, name, n):
        return [self.sem(f"{name}{i}") for i in range(n)]

    def close(self):
        self.nc.clear_and_free_semaphores(self.taken)
        self.nc.all_engine_barrier()


def conditioning(nc, io, keep, scratch):
    with ExitStack() as ctx:
        k = Scope(nc, ctx, "c_")
        uv = k.sb("uv", [P, KC, 2 * R])
        uvt = k.sb("uvt", [2 * R, D])
        row = k.sb("row", [2 * R, D])
        sq_junk = k.sb("sq_junk", [2 * R, D])
        dot_junk = k.sb("dot_junk", [2 * R, D])
        norm2 = k.sb("norm2", [2 * R, 1])
        norm = k.sb("norm", [2 * R, 1])
        dot = k.sb("dot", [2 * R, 1])
        normeps = k.sb("normeps", [2 * R, 1])
        coef = k.sb("coef", [2 * R, 2])
        inv = k.sb("inv", [2 * R, R])
        own = k.sb("own", [2 * R, 1])
        eye = k.sb("eye", [2 * R, R])
        later = k.sb("later", [2 * R, R])
        basis = k.sb("basis", [P, KC, 2 * R])
        vtv = k.sb("vtv", [R, R])
        core4 = k.sb("core4", [R, P])
        rw = k.sb("rw", [P, KC, R])
        rw4 = k.sb("rw4", [P, KC, 4 * R])
        w1 = k.sb("w1", [P, D])
        w1t = k.sb("w1t", [P, KC, P])
        wada = k.sb("wada", [P, KC, 2 * D])
        bada = k.sb("bada", [P, 2 * D])
        xin = k.sb("xin", [P, 2, NQT, D])
        sums = k.sb("sums", [1, B, D])
        pooled = k.sb("pooled", [P, KC * B])
        hid = k.sb("hid", [P, B])
        gw2 = k.sb("gw2", [P, 1])
        gb1 = k.sb("gb1", [P, 1])
        gb2 = k.sb("gb2", [P, 1])
        safety = k.sb("safety", [P, B])
        gate = k.sb("gate", [P, 2, B])
        cond = k.sb("cond", [P, B, CW])
        rbias = k.sb("rbias", [P, 2, D])
        tok = k.sb("tok", [P, B], I32)
        tokf = k.sb("tokf", [P, 2, B])
        freq = k.sb("freq", [P, 2])
        angle = k.sb("angle", [P, 2, B])
        turns = k.sb("turns", [P, 4, B])
        arg = k.sb("arg", [P, 4, B])
        emb = k.sb("emb", [P, 4, B])
        ones = k.sb("ones", [P, 1])
        wraw = k.sb("wraw", [P, D * 2])

        p_uv = k.ps("p_uv", [P, 512])
        p_ada = [k.ps(f"p_ada{i}", [P, 512]) for i in range(2)]
        p_sum = [k.ps(f"p_sum{i}", [P, 512]) for i in range(2)]
        p_w1 = k.ps("p_w1", [P, 512])
        p_rw = k.ps("p_rw", [P, 512])
        p_small = k.ps("p_small", [P, 512])

        uv_in, rw_in, tok_in, freq_in, ada_in, bada_in = (k.sem(n) for n in ("uv_in", "rw_in", "tok_in", "freq_in", "ada_in", "bada_in"))
        w1_in, gate_in, rb_in, wraw_in = (k.sem(n) for n in ("w1_in", "gate_in", "rb_in", "wraw_in"))
        x_in = k.sems("x_in", 2)
        ident_set, eye_set, later_set, ones_set, rw4_set = (k.sem(n) for n in ("ident_set", "eye_set", "later_set", "ones_set", "rw4_set"))
        uvt_ps, uvt_set, row_set, norm_set = (k.sem(n) for n in ("uvt_ps", "uvt_set", "row_set", "norm_set"))
        arg_set, emb_set, ada_ps, ada_out, ada_added = (k.sem(n) for n in ("arg_set", "emb_set", "ada_ps", "ada_out", "ada_added"))
        w1t_ps, w1t_set, rw_ps, rw_hi, sum_ps, sum_set = (k.sem(n) for n in ("w1t_ps", "w1t_set", "rw_ps", "rw_hi", "sum_ps", "sum_set"))
        pooled_ps, pooled_set, hid_ps, hid_set, gate_ps, gate_set = (k.sem(n) for n in ("pooled_ps", "pooled_set", "hid_ps", "hid_set", "gate_ps", "gate_set"))
        ortho, basis_ps, basis_set, vtv_ps, vtv_set, core_ps, core_set, m_ps = (
            k.sem(n) for n in ("ortho", "basis_ps", "basis_set", "vtv_ps", "vtv_set", "core_ps", "core_set", "m_ps"))
        rb_set, done, stored, split_done = (k.sem(n) for n in ("rb_set", "done", "stored", "split_done"))
        dve_own, act_own, pool_own = (k.sem(n) for n in ("dve_own", "act_own", "pool_own"))

        ctx.callback(k.close)
        block = ctx.enter_context(nc.Block())
        splits = [(src, c0) for src in range(3) for c0 in range(0, KC, 2)]

        @block.sync
        def _(sp):
            for half, w in enumerate((io["L0_cond_U"], io["L0_cond_V"])):
                sp.dma_start(uv[:, :, half * R:(half + 1) * R], w.rearrange("(c p) r -> p c r", p=P)).then_inc(uv_in, 16)
            sp.dma_start(tok[:, :], io["itok_B_34_63"].partition_broadcast(P)).then_inc(tok_in, 16)
            sp.dma_start(freq[:, :], io["freq"]).then_inc(freq_in, 16)
            sp.dma_start(wada[:, :, :], io["L1_cond_W_ada"].rearrange("(c p) n -> p c n", p=P)).then_inc(ada_in, 16)
            sp.dma_start(bada[:, :], io["L1_cond_b_ada"].partition_broadcast(P)).then_inc(bada_in, 16)
            sp.dma_start(rw[:, :, :], io["L0_cond_resp_w"].rearrange("(c p) r -> p c r", p=P)).then_inc(rw_in, 16)
            sp.dma_start(w1[:, :], io["L0_cond_gate_w1"]).then_inc(w1_in, 16)
            sp.dma_start(gw2[:, :], io["L0_cond_gate_w2"].rearrange("o p -> p o")).then_inc(gate_in, 16)
            sp.dma_start(gb1[:, :], io["L0_cond_gate_b1"].rearrange("(p o) -> p o", o=1)).then_inc(gate_in, 16)
            sp.dma_start(gb2[:, :], io["L0_cond_gate_b2"].partition_broadcast(P)).then_inc(gate_in, 16)
            sp.dma_start(safety[:, :], io["condB_safetyscore"].partition_broadcast(P)).then_inc(gate_in, 16)
            sp.dma_start(rbias[:, 0, :], io["L0_cond_resp_b"].partition_broadcast(P)).then_inc(rb_in, 16)
            sp.dma_start(rbias[:, 1, :], io["L0_cond_safety_bias"].partition_broadcast(P)).then_inc(rb_in, 16)
            for b in range(B):
                if b >= 2:
                    sp.wait_ge(sum_ps, b - 1)
                sp.dma_start(xin[:, b % 2], io["x"][b].rearrange("(t p) d -> p t d", p=P)).then_inc(x_in[b % 2], 16)
            for n, (src, c0) in enumerate(splits):
                w = (io["L1_cond_Wq"], io["L1_cond_Wk"], io["L1_cond_Wv"])[src]
                if n:
                    sp.wait_ge(split_done, n)
                sp.dma_start(wraw[:, :].rearrange("p (c n) -> p c n", c=2),
                             w.rearrange("(c p) n -> p c n", p=P)[:, c0:c0 + 2, :]).then_inc(wraw_in, 16)
            sp.wait_ge(done, 1)
            sp.dma_start(scratch["cond"].rearrange("b p n -> p b n"), cond[:, :, :]).then_inc(stored, 16)
            sp.wait_ge(stored, 16)

        @block.gpsimd
        def _(pool):
            link = chain_on(pool, pool_own)
            ident = keep["ident"]
            link(pool.memset(ident[:, :], 0.0))
            pool.affine_select(out=ident[:, :], in_=ident[:, :], compare_op=ALU.not_equal, fill=1.0,
                               base=0, pattern=[[-1, P]], channel_multiplier=1).then_inc(ident_set, 1)
            link(pool.memset(eye[:, :], 0.0))
            link(pool.memset(later[:, :], -1.0))
            for q in range(2):
                pool.affine_select(out=eye[q * R:(q + 1) * R, :], in_=eye[q * R:(q + 1) * R, :], compare_op=ALU.not_equal,
                                   fill=1.0, base=0, pattern=[[-1, R]], channel_multiplier=1).then_inc(eye_set, 1)
                pool.wait_ge(eye_set, q + 1)
                pool.affine_select(out=later[q * R:(q + 1) * R, :], in_=later[q * R:(q + 1) * R, :], compare_op=ALU.is_gt,
                                   fill=0.0, base=0, pattern=[[-1, R]], channel_multiplier=1).then_inc(later_set, 1)
                pool.wait_ge(later_set, q + 1)
            link(pool.memset(ones[:, :], 1.0))
            link(pool.memset(keep["neghalf"][:, :], -0.5))
            link(pool.memset(keep["eps"][:, :], LN_EPS))
            link(pool.memset(cond[:, :, 3 * D:CW], 0.0))
            pool.wait_ge(ident_set, 1)
            pool.tensor_copy(keep["identb"][:, :], ident[:, :]).then_inc(ones_set, 1)
            pool.wait_ge(ones_set, 1)
            pool.wait_ge(rw_in, 16)
            for q in range(4):
                pool.tensor_copy(rw4[:, :, q * R:(q + 1) * R], rw[:, :, :]).then_inc(rw4_set, 1)
                pool.wait_ge(rw4_set, q + 1)
            pool.wait_ge(bada_in, 16)
            link(pool.tensor_scalar(bada[:, 0:D], bada[:, 0:D], 1.0, None, ALU.add))
            pool.wait_ge(rb_in, 32)
            pool.tensor_tensor(rbias[:, 0, :], rbias[:, 0, :], rbias[:, 1, :], ALU.add).then_inc(rb_set, 1)
            for n in range(2 * B):
                b, half = divmod(n, 2)
                pool.wait_ge(ada_out, n + 1)
                part = cond[:, b, half * D:(half + 1) * D]
                pool.tensor_tensor(part, part, bada[:, half * D:(half + 1) * D], ALU.add).then_inc(ada_added, 1)
            for n, (src, c0) in enumerate(splits):
                pool.wait_ge(wraw_in, 16 * (n + 1))
                hi, lo = keep["wqkv"][src]
                raw = wraw[:, :].rearrange("p (c n) -> p c n", c=2)
                link(pool.tensor_copy(hi[:, c0:c0 + 2, :], raw))
                pool.tensor_tensor(lo[:, c0:c0 + 2, :], raw, hi[:, c0:c0 + 2, :].bitcast(F32), ALU.subtract).then_inc(split_done, 1)

        @block.tensor
        def _(pe):
            ident = keep["ident"][:, :]
            pe.wait_ge(ident_set, 1)
            pe.wait_ge(uv_in, 32)
            for c in range(KC):
                last = pe.transpose(p_uv[0:2 * R, c * P:(c + 1) * P], uv[:, c, :], ident)
            last.then_inc(uvt_ps, 1)
            pe.wait_ge(emb_set, 1)
            pe.wait_ge(ada_in, 16)
            for n in range(2 * B):
                b, half = divmod(n, 2)
                if n >= 2:
                    pe.wait_ge(ada_out, n - 1)
                for c in range(KC):
                    last = pe.matmul(p_ada[n % 2][:, :], emb[:, c, b:b + 1].to_broadcast([P, P]),
                                     wada[:, c, half * D:(half + 1) * D], start=c == 0, stop=c == KC - 1)
                last.then_inc(ada_ps, 1)
            pe.wait_ge(w1_in, 16)
            for c in range(KC):
                last = pe.transpose(p_w1[:, c * P:(c + 1) * P], w1[:, c * P:(c + 1) * P], ident)
            last.then_inc(w1t_ps, 1)
            pe.wait_ge(rw4_set, 4)
            for c in range(KC):
                last = pe.transpose(p_rw[:, c * P:(c + 1) * P], rw4[:, c, :], ident)
            last.then_inc(rw_ps, 1)
            pe.wait_ge(ones_set, 1)
            for b in range(B):
                pe.wait_ge(x_in[b % 2], 16 * (b // 2 + 1))
                if b >= 2:
                    pe.wait_ge(sum_set, b - 1)
                for t in range(NQT):
                    last = pe.matmul(p_sum[b % 2][0:1, :], ones[:, :], xin[:, b % 2, t, :], start=t == 0, stop=t == NQT - 1)
                last.then_inc(sum_ps, 1)
            pe.wait_ge(sum_set, B)
            for c in range(KC):
                for b in range(B):
                    last = pe.matmul(p_small[:, c * B + b:c * B + b + 1], sums[0:1, b, c * P:(c + 1) * P], ones[0:1, 0:1],
                                     start=True, stop=True)
            last.then_inc(pooled_ps, 1)
            pe.wait_ge(pooled_set, 1)
            pe.wait_ge(w1t_set, 1)
            for c in range(KC):
                last = pe.matmul(p_small[:, 32:32 + B], w1t[:, c, :], pooled[:, c * B:(c + 1) * B], start=c == 0, stop=c == KC - 1)
            last.then_inc(hid_ps, 1)
            pe.wait_ge(hid_set, 1)
            pe.wait_ge(gate_in, 64)
            pe.matmul(p_small[:, 64:64 + B], gw2[:, 0:1].to_broadcast([P, P]), hid[:, :], start=True, stop=True).then_inc(gate_ps, 1)
            pe.wait_ge(ortho, 1)
            for c in range(KC):
                last = pe.transpose(p_uv[:, c * 2 * R:(c + 1) * 2 * R], uvt[:, c * P:(c + 1) * P], keep["ident"][0:2 * R, 0:2 * R])
            last.then_inc(basis_ps, 1)
            pe.wait_ge(basis_set, 1)
            pe.wait_ge(ada_out, 2 * B)
            for c in range(KC):
                last = pe.matmul(p_ada[0][0:R, 0:R], basis[:, c, R:2 * R], basis[:, c, R:2 * R], start=c == 0, stop=c == KC - 1)
            last.then_inc(vtv_ps, 1)
            pe.wait_ge(vtv_set, 1)
            pe.matmul(p_ada[1][0:R, 0:R], vtv[:, :], uvt[0:R, 0:R], start=True, stop=True).then_inc(core_ps, 1)
            pe.wait_ge(core_set, 1)
            for c in range(KC):
                last = pe.matmul(p_uv[:, c * P:(c + 1) * P], uvt[0:R, c * P:(c + 1) * P], core4[:, :], start=True, stop=True)
            last.then_inc(m_ps, 1)

        @block.scalar
        def _(act):
            act.wait_ge(arg_set, 1)
            act.activation(turns[:, :, :], arg[:, :, :], ACT.Sin).then_inc(act_own, 1)
            act.wait_ge(act_own, 1)
            act.activation(emb[:, :, :], turns[:, :, :], ACT.Silu).then_inc(emb_set, 1)
            for i in range(R):
                act.wait_ge(row_set, i + 1)
                act.activation(sq_junk[:, :], row[:, :], ACT.Square, accum_out=norm2[:, :]).then_inc(act_own, 1)
                act.wait_ge(act_own, i + 2)
                act.activation(norm[:, :], norm2[:, :], ACT.Sqrt).then_inc(norm_set, 1)
                if 1 <= i <= 2 * B:
                    b, half = divmod(i - 1, 2)
                    act.wait_ge(ada_ps, i)
                    act.activation(cond[:, b, half * D:(half + 1) * D], p_ada[(i - 1) % 2][:, :], ACT.Copy).then_inc(ada_out, 1)
                if i == 10:
                    act.wait_ge(w1t_ps, 1)
                    act.activation(w1t[:, :, :], p_w1[:, :].rearrange("p (c n) -> p c n", c=KC), ACT.Copy).then_inc(w1t_set, 1)
                if i == 11:
                    act.wait_ge(rw_ps, 1)
                    act.activation(keep["rw"][:, :], p_rw[:, :], ACT.Copy).then_inc(rw_hi, 1)
                if i in (14, 18, 22, 26):
                    b = (i - 14) // 4
                    act.wait_ge(sum_ps, b + 1)
                    act.activation(sums[0:1, b, :], p_sum[b % 2][0:1, :], ACT.Copy).then_inc(sum_set, 1)
                if i == 28:
                    act.wait_ge(pooled_ps, 1)
                    act.activation(pooled[:, :], p_small[:, 0:KC * B], ACT.Copy).then_inc(pooled_set, 1)
                if i == 30:
                    act.wait_ge(hid_ps, 1)
                    act.wait_ge(gate_in, 64)
                    act.activation(hid[:, :], p_small[:, 32:32 + B], ACT.Relu, bias=gb1[:, :], scale=1.0 / S).then_inc(hid_set, 1)
            act.wait_ge(gate_ps, 1)
            act.activation(gate[:, 0, :], p_small[:, 64:64 + B], ACT.Sigmoid, bias=gb2[:, :]).then_inc(gate_set, 1)
            act.activation(gate[:, 1, :], safety[:, :], ACT.Sigmoid).then_inc(gate_set, 1)

        @block.vector
        def _(dve):
            link = chain_on(dve, dve_own)
            dve.wait_ge(tok_in, 16)
            dve.wait_ge(freq_in, 16)
            link(dve.tensor_copy(tokf[:, 0, :], tok[:, :]))
            link(dve.tensor_scalar(tokf[:, 1, :], tokf[:, 0, :], 0.01, 4000.0, ALU.mult, ALU.mult))
            for c in range(2):
                link(dve.tensor_scalar(angle[:, c, :], tokf[:, 1, :], freq[:, c:c + 1], None, ALU.mult))
            for q, quarter in enumerate((0.0, 0.25)):
                t, a = turns[:, 2 * q:2 * q + 2, :], arg[:, 2 * q:2 * q + 2, :]
                link(dve.tensor_scalar(t, angle[:, :, :], 1.0 / (2 * math.pi), quarter, ALU.mult, ALU.add))
                link(dve.tensor_scalar(t, t, ROUND, -ROUND, ALU.add, ALU.add))
                link(dve.scalar_tensor_tensor(a, t, -TWO_PI[0], angle[:, :, :], ALU.mult, ALU.add))
                link(dve.scalar_tensor_tensor(a, t, -TWO_PI[1], a, ALU.mult, ALU.add))
                link(dve.scalar_tensor_tensor(a, t, -TWO_PI[2], a, ALU.mult, ALU.add))
                link(dve.tensor_scalar(a, a, quarter * 2 * math.pi, PI_MAX, ALU.add, ALU.min))
                last = dve.tensor_scalar(a, a, -PI_MAX, None, ALU.max)
                if q == 0:
                    link(last)
            last.then_inc(arg_set, 1)

            dve.wait_ge(uvt_ps, 1)
            link(dve.tensor_copy(uvt[:, :], p_uv[0:2 * R, :]))
            dve.wait_ge(eye_set, 2)
            dve.wait_ge(later_set, 2)
            for i in range(R):
                dve.stream_shuffle(row[:, :], uvt[:, :], [i] * R).then_inc(row_set, 1)
                dve.wait_ge(row_set, i + 1)
                link(dve.tensor_tensor_reduce(dot_junk[:, :], row[:, :], uvt[:, :], 1.0, 0.0, ALU.mult, ALU.add, dot[:, :]))
                link(dve.tensor_scalar(coef[:, 0:1], later[:, i:i + 1], dot[:, 0:1], None, ALU.mult))
                dve.wait_ge(norm_set, i + 1)
                link(dve.tensor_scalar(normeps[:, :], norm[:, :], 1e-8, None, ALU.add))
                link(dve.reciprocal(inv[:, i:i + 1], normeps[:, :]))
                link(dve.tensor_scalar(coef[:, 1:2], coef[:, 0:1], inv[:, i:i + 1], inv[:, i:i + 1], ALU.mult, ALU.mult))
                link(dve.scalar_tensor_tensor(uvt[:, :], row[:, :], coef[:, 1:2], uvt[:, :], ALU.mult, ALU.add))
            link(dve.tensor_tensor_reduce(dot_junk[:, 0:R], inv[:, :], eye[:, :], 1.0, 0.0, ALU.mult, ALU.add, own[:, :]))
            dve.tensor_scalar(uvt[:, :], uvt[:, :], own[:, 0:1], None, ALU.mult).then_inc(ortho, 1)
            dve.wait_ge(basis_ps, 1)
            dve.tensor_copy(basis[:, :, :], p_uv[:, 0:KC * 2 * R].rearrange("p (c r) -> p c r", c=KC)).then_inc(basis_set, 1)
            dve.wait_ge(vtv_ps, 1)
            dve.tensor_copy(vtv[:, :], p_ada[0][0:R, 0:R]).then_inc(vtv_set, 1)
            dve.wait_ge(core_ps, 1)
            dve.tensor_copy(core4[:, :].rearrange("p (q r) -> p q r", q=4),
                            p_ada[1][0:R, 0:R].unsqueeze(1).to_broadcast([R, 4, R])).then_inc(core_set, 1)
            dve.wait_ge(rw_hi, 1)
            for q in (1, 3):
                rows = slice(q * R, (q + 1) * R)
                link(dve.tensor_tensor(keep["rw"][rows, :], p_rw[rows, :], keep["rw"][rows, :].bitcast(F32), ALU.subtract))
            dve.wait_ge(m_ps, 1)
            link(dve.tensor_copy(keep["m4"][:, :, :], p_uv[:, :].rearrange("p (c n) -> p c n", c=KC)))
            dve.wait_ge(gate_set, 2)
            dve.wait_ge(ones_set, 1)
            link(dve.tensor_tensor(cond[:, :, 3 * D:3 * D + 1], gate[:, 0, :].unsqueeze(2), gate[:, 1, :].unsqueeze(2), ALU.mult))
            dve.wait_ge(rb_set, 1)
            for b in range(B):
                link(dve.tensor_scalar(cond[:, b, 2 * D:3 * D], rbias[:, 0, :], cond[:, b, 3 * D:3 * D + 1], None, ALU.mult))
            dve.wait_ge(ada_added, 2 * B)
            dve.tensor_copy(coef[:, 0:1], own[:, :]).then_inc(done, 1)


def projections(nc, io, keep, scratch):
    with ExitStack() as ctx:
        k = Scope(nc, ctx, "a_")
        x = k.sb("x", [P, NT, D])
        xt = k.sb("xt", [P, KC, TB])
        feat = k.sb("feat", [P, TB], F32R)
        y = k.sb("y", [P, NT, D])
        xo = k.sb("xo", [P, NT, D])
        stats = k.sb("stats", [P, NT, 6])
        meanvar = k.sb("meanvar", [P, NT, 2])
        rstd = k.sb("rstd", [P, NT, 2])
        xm_hi = k.sb("xm_hi", [P, KC, TB], F32R)
        xm_lo = k.sb("xm_lo", [P, KC, TB], F32R)
        out_f = k.sb("out_f", [P, RING, TB])
        out_hi = k.sb("out_hi", [P, RING, TB], F32R)
        out_lo = k.sb("out_lo", [P, RING, TB], F32R)
        v = k.sb("v", [P, 2, D])
        cond = k.sb("cond", [P, CW])
        bias_v = k.sb("bias_v", [P, D])
        bias_o = k.sb("bias_o", [P, D])
        bias_qk = k.sb("bias_qk", [P, 2, KC])
        mask8 = k.sb("mask8", [P, 2, S], U8)
        maskb = k.sb("maskb", [P, 2, S], BF16)

        p_out = [k.ps(f"p_out{i}", [P, 512]) for i in range(3)]
        p_t = [k.ps(f"p_t{i}", [P, 512]) for i in range(2)]
        p_feat = k.ps("p_feat", [P, 512])
        p_resp = [k.ps(f"p_resp{i}", [P, 512]) for i in range(2)]

        x_in, cond_in, bias_in = k.sem("x_in"), k.sem("cond_in"), k.sem("bias_in")
        mask_in, mask_out = k.sems("mask_in", 2), k.sems("mask_out", 2)
        qk_out, v_out, xo_out = k.sems("qk_out", RING), k.sems("v_out", 2), k.sem("xo_out")
        xt_ps, xt_set, feat_ps, feat_hi, feat_set, resp_ps = (k.sem(n) for n in ("xt_ps", "xt_set", "feat_ps", "feat_hi", "feat_set", "resp_ps"))
        xs_set, y_set, bn_set, stats_set, eps_set, rstd_set = (k.sem(n) for n in ("xs_set", "y_set", "bn_set", "stats_set", "eps_set", "rstd_set"))
        ln_set, scaled_set, xm_set, xo_set, xmt_ps, hi_set, lo_set = (
            k.sem(n) for n in ("ln_set", "scaled_set", "xm_set", "xo_set", "xmt_ps", "hi_set", "lo_set"))
        out_ps, qk_act, qk_lo, v_set, bq_set, mask_set = (k.sem(n) for n in ("out_ps", "qk_act", "qk_lo", "v_set", "bq_set", "mask_set"))
        ctx.callback(k.close)
        block = ctx.enter_context(nc.Block())

        NQK = 2 * KC
        NOUT = NQK + NT
        scale = 1.0 / math.sqrt(HD)
        x_blk = io["x"].rearrange("b (n t p) d -> (b n) p t d", t=NT, p=P)
        xo_blk = scratch["xo"].rearrange("(n t p) d -> n p t d", t=NT, p=P)
        mask_blk = io["mask_Bx1xSxS_bk0"].rearrange("b o (t p) k -> (b o t) p k", p=P)
        stacks = [scratch[n].rearrange("(m g) r s n -> m g r s n", g=KC) for n in ("q", "k")]
        hi_parts = (slice(0, 2), slice(0, 4, 2))
        lo_parts = (slice(2, 4), slice(1, 4, 2))
        v_blk = scratch["v"].rearrange("(m g) p t c -> m t p g c", g=KC)

        def slots(eng, prologue, slot):
            prologue(0)
            slot(0, False)
            with eng.Fori(1, NBLK - 1) as m:
                slot(m, False)
            slot(NBLK - 1, True)

        @block.sync
        def _(sp):
            sp.dma_start(bias_v[:, :], io["L1_cond_bv"].partition_broadcast(P)).then_inc(bias_in, 16)
            sp.dma_start(bias_o[:, :], io["L1_cond_bo"].partition_broadcast(P)).then_inc(bias_in, 16)
            sp.dma_start(bias_qk[:, 0, :], io["L1_cond_bq"].rearrange("(c p) -> p c", p=P)).then_inc(bias_in, 16)
            sp.dma_start(bias_qk[:, 1, :], io["L1_cond_bk"].rearrange("(c p) -> p c", p=P)).then_inc(bias_in, 16)

            def load(n):
                at_least(sp, y_set, NT * n)
                sp.dma_start(x[:, :, :], x_blk[n]).then_inc(x_in, 16)

            def load_cond(n, b):
                at_least(sp, xm_set, NT * n)
                sp.dma_start(cond[:, :], scratch["cond"][b]).then_inc(cond_in, 16)

            def store_xo(n):
                sp.wait_ge(xo_set, NT * (n + 1))
                sp.dma_start(xo_blk[n], xo[:, :, :]).then_inc(xo_out, 16)

            def slot(m, last):
                for i in range(NQK):
                    side, g = divmod(i, KC)
                    sp.wait_ge(qk_act, NQK * m + i + 1)
                    hi = out_hi[:, i % RING, :].bitcast(F32).unsqueeze(1).to_broadcast([P, 2, TB])
                    sp.dma_start(stacks[side][m, g][:, hi_parts[side], :], hi).then_inc(qk_out[i % RING], 16)
                    sp.wait_ge(qk_lo, NQK * m + i + 1)
                    lo = out_lo[:, i % RING, :].bitcast(F32).unsqueeze(1).to_broadcast([P, 2, TB])
                    sp.dma_start(stacks[side][m, g][:, lo_parts[side], :], lo).then_inc(qk_out[i % RING], 16)
                more = not last and not (isinstance(m, int) and m == NBLK - 2)
                if more:
                    load(m + 2)
                for t in range(NT):
                    sp.wait_ge(v_set, NT * m + t + 1)
                    sp.dma_start(v_blk[m, t], v[:, t % 2, :].rearrange("p (g c) -> p g c", g=KC)).then_inc(v_out[t % 2], 16)
                if more:
                    load_cond(m + 2, (m + 2) // 2)
                if not last:
                    store_xo(m + 1)

            load(0)
            load_cond(0, 0)
            load(1)
            load_cond(1, 0)
            store_xo(0)
            slot(0, False)
            with sp.Fori(1, NBLK - 2) as m:
                slot(m, False)
            slot(NBLK - 2, False)
            slot(NBLK - 1, True)
            for i in range(RING):
                sp.wait_ge(qk_out[i], 32 * NBLK * NQK // RING)
            for i in range(2):
                sp.wait_ge(v_out[i], 16 * NBLK * NT // 2)
            sp.wait_ge(xo_out, 16 * NBLK)

        @block.gpsimd
        def _(pool):
            def mask_load(i, buf):
                pool.dma_start(mask8[:, buf, :], mask_blk[i]).then_inc(mask_in[buf], 16)

            def front(n):
                pool.wait_ge(cond_in, 16 * (n + 1))
                pool.wait_ge(x_in, 16 * (n + 1))
                pool.wait_ge(xt_ps, KC * (n + 1))
                for t in range(NT):
                    pool.tensor_tensor(x[:, t, :], x[:, t, :], cond[:, 2 * D:3 * D], ALU.add).then_inc(xs_set, 1)
                for t in range(NT):
                    pool.wait_ge(stats_set, NT * n + t + 1)
                    pool.tensor_tensor(rstd[:, t, 0:1], meanvar[:, t, 1:2], keep["eps"][:, :], ALU.add).then_inc(eps_set, 1)
                    pool.wait_ge(eps_set, NT * n + t + 1)
                    pool.tensor_tensor(rstd[:, t, 1:2], rstd[:, t, 0:1], keep["neghalf"][:, :], ALU.pow).then_inc(rstd_set, 1)

            def masks(m):
                for i in range(4):
                    buf = i % 2
                    loaded, stored = counted(pool, 32 * m + 16 * (i // 2 + 1)), counted(pool, 32 * m + 16 * (i // 2))
                    carried(pool, mask_in[buf])
                    pool.wait_ge(mask_in[buf], loaded)
                    at_least(pool, mask_out[buf], stored)
                    pool.tensor_scalar(maskb[:, buf, :], mask8[:, buf, :], MASKED, None, ALU.mult).then_inc(mask_set, 1)
                    pool.wait_ge(mask_set, 4 * m + i + 1)
                    pool.dma_start(scratch["mask"][4 * m + i], maskb[:, buf, :]).then_inc(mask_out[buf], 16)
                    if not (isinstance(m, int) and m == NBLK - 1 and i >= 2):
                        mask_load(4 * m + i + 2, buf)

            mask_load(0, 0)
            mask_load(1, 1)
            front(0)
            front(1)
            masks(0)
            with pool.Fori(1, NBLK - 1) as m:
                front(m + 1)
                masks(m)
            masks(NBLK - 1)
            for buf in range(2):
                pool.wait_ge(mask_out[buf], 32 * NBLK)

        @block.tensor
        def _(pe):
            ident = keep["ident"][:, :]

            def transpose_x(n, c):
                if c == 0:
                    pe.wait_ge(x_in, 16 * (n + 1))
                if c < 2:
                    at_least(pe, lo_set, KC * n - 1 + c)
                else:
                    pe.wait_ge(xt_set, KC * n + c - 1)
                for t in range(NT):
                    last = pe.transpose(p_t[c % 2][:, t * P:(t + 1) * P], x[:, t, c * P:(c + 1) * P], ident)
                last.then_inc(xt_ps, 1)

            def features(n):
                pe.wait_ge(xt_set, KC * (n + 1))
                at_least(pe, feat_set, n)
                for c in range(KC):
                    last = pe.matmul(p_feat[:, :], keep["m4"][:, c, :], xt[:, c, :], start=c == 0, stop=c == KC - 1)
                last.then_inc(feat_ps, 1)

            def response(n, t):
                pe.wait_ge(feat_set, n + 1)
                at_least(pe, y_set, NT * n + t - 1)
                pe.matmul(p_resp[t % 2][:, :], feat[:, t * P:(t + 1) * P], keep["rw"][:, :], start=True, stop=True).then_inc(resp_ps, 1)

            def transpose_xm(n, c):
                if c == 0:
                    pe.wait_ge(xm_set, NT * (n + 1))
                if c < 2:
                    pe.wait_ge(xt_set, KC * n + 3 + c)
                else:
                    pe.wait_ge(lo_set, KC * n + c - 1)
                for t in range(NT):
                    last = pe.transpose(p_t[c % 2][:, t * P:(t + 1) * P], y[:, t, c * P:(c + 1) * P], ident)
                last.then_inc(xmt_ps, 1)

            def output(m, i):
                bank = i % 3
                before = i - 3
                if before >= NQK:
                    pe.wait_ge(v_set, NT * m + before - NQK + 1)
                elif before >= 0:
                    pe.wait_ge(qk_act, NQK * m + before + 1)
                else:
                    at_least(pe, v_set, NT * m + before + 1)
                if i == 0:
                    pe.wait_ge(lo_set, KC * (m + 1))
                out = p_out[bank][:, :]
                if i < NQK:
                    side, j = divmod(i, KC)
                    w_hi, w_lo = keep["wqkv"][side]
                    cols = slice(j * P, (j + 1) * P)
                    parts = [((w_hi[:, c, cols], xm_hi[:, c, :]), (w_hi[:, c, cols], xm_lo[:, c, :]), (w_lo[:, c, cols], xm_hi[:, c, :]))
                             for c in range(KC)]
                else:
                    w_hi, w_lo = keep["wqkv"][2]
                    cols = slice((i - NQK) * P, (i - NQK + 1) * P)
                    parts = [((xm_hi[:, c, cols], w_hi[:, c, :]), (xm_hi[:, c, cols], w_lo[:, c, :]), (xm_lo[:, c, cols], w_hi[:, c, :]))
                             for c in range(KC)]
                products = [pair for three in parts for pair in three]
                for n, (left, right) in enumerate(products):
                    last = pe.matmul(out, left, right, start=n == 0, stop=n == len(products) - 1)
                last.then_inc(out_ps, 1)

            def front(n):
                for c in range(KC):
                    transpose_x(n, c)
                features(n)
                for t in range(NT):
                    response(n, t)
                for c in range(KC):
                    transpose_xm(n, c)

            def slot(m, last):
                for i in range(NOUT):
                    output(m, i)
                    if last:
                        continue
                    if i < 2:
                        transpose_x(m + 1, 2 * i)
                        transpose_x(m + 1, 2 * i + 1)
                    if i == 2:
                        features(m + 1)
                    if 4 <= i < 4 + NT:
                        response(m + 1, i - 4)
                if not last:
                    for c in range(KC):
                        transpose_xm(m + 1, c)

            slots(pe, front, slot)

        @block.scalar
        def _(act):
            act.wait_ge(bias_in, 64)
            act.activation(bias_qk[:, 0, :], bias_qk[:, 0, :], ACT.Copy, scale=scale).then_inc(bq_set, 1)
            act.wait_ge(bq_set, 1)

            def empty_xt(n, c):
                act.wait_ge(xt_ps, KC * n + c + 1)
                at_least(act, feat_ps, n)
                act.activation(xt[:, c, :], p_t[c % 2][:, :], ACT.Copy).then_inc(xt_set, 1)

            def high(n, c):
                act.wait_ge(xmt_ps, KC * n + c + 1)
                at_least(act, out_ps, NOUT * n)
                act.activation(xm_hi[:, c, :], p_t[c % 2][:, :], ACT.Copy).then_inc(hi_set, 1)

            def front(n):
                for c in range(KC):
                    empty_xt(n, c)
                for c in range(KC):
                    high(n, c)

            def slot(m, last):
                for i in range(NOUT):
                    if i < NQK:
                        side, j = divmod(i, KC)
                        r = i % RING
                        act.wait_ge(out_ps, NOUT * m + i + 1)
                        at_least(act, qk_out[r], 32 * (NQK // RING * m + i // RING))
                        bias = bias_qk[:, side, j:j + 1]
                        act.activation(out_f[:, r, :], p_out[i % 3][:, :], ACT.Identity, bias=bias, scale=(scale, 1.0)[side])
                        act.activation(out_hi[:, r, :], p_out[i % 3][:, :], ACT.Identity, bias=bias, scale=(scale, 1.0)[side]).then_inc(qk_act, 1)
                    if i < 2 and not last:
                        empty_xt(m + 1, 2 * i)
                        empty_xt(m + 1, 2 * i + 1)
                if not last:
                    for c in range(KC):
                        high(m + 1, c)

            slots(act, front, slot)

        @block.vector
        def _(dve):
            dve.wait_ge(bias_in, 64)

            def cut_features(n):
                dve.wait_ge(feat_ps, n + 1)
                at_least(dve, resp_ps, NT * n)
                dve.tensor_copy(feat[:, :], p_feat[:, :]).then_inc(feat_hi, 1)
                dve.wait_ge(feat_hi, n + 1)
                low = slice(2 * R, 4 * R)
                dve.tensor_tensor(feat[low, :], p_feat[low, :], feat[low, :].bitcast(F32), ALU.subtract).then_inc(feat_set, 1)

            def condition(n, t):
                tile = NT * n + t + 1
                dve.wait_ge(resp_ps, tile)
                dve.wait_ge(xs_set, tile)
                if t == 0:
                    at_least(dve, xmt_ps, KC * n)
                dve.scalar_tensor_tensor(y[:, t, :], p_resp[t % 2][:, :], cond[:, 3 * D:3 * D + 1], x[:, t, :],
                                         ALU.mult, ALU.add).then_inc(y_set, 1)
                dve.wait_ge(y_set, tile)
                dve.bn_stats(stats[:, t, :], y[:, t, :]).then_inc(bn_set, 1)
                carried(dve, bn_set)
                dve.wait_ge(bn_set, tile)
                dve.bn_aggr(meanvar[:, t, :], stats[:, t, :]).then_inc(stats_set, 1)

            def modulate(n, t):
                tile = NT * n + t + 1
                dve.wait_ge(rstd_set, tile)
                dve.wait_ge(stats_set, tile)
                dve.tensor_scalar(y[:, t, :], y[:, t, :], meanvar[:, t, 0:1], rstd[:, t, 1:2], ALU.subtract, ALU.mult).then_inc(ln_set, 1)
                dve.wait_ge(ln_set, tile)
                dve.tensor_tensor(y[:, t, :], y[:, t, :], cond[:, 0:D], ALU.mult).then_inc(scaled_set, 1)
                dve.wait_ge(scaled_set, tile)
                dve.tensor_tensor(y[:, t, :], y[:, t, :], cond[:, D:2 * D], ALU.add).then_inc(xm_set, 1)
                dve.wait_ge(xm_set, tile)
                if t == 0:
                    at_least(dve, xo_out, 16 * n)
                dve.tensor_tensor(xo[:, t, :], y[:, t, :], bias_o[:, :], ALU.add).then_inc(xo_set, 1)

            def low(n, c):
                dve.wait_ge(hi_set, KC * n + c + 1)
                dve.tensor_tensor(xm_lo[:, c, :], p_t[c % 2][:, :], xm_hi[:, c, :].bitcast(F32), ALU.subtract).then_inc(lo_set, 1)

            def front(n):
                cut_features(n)
                for t in range(NT):
                    condition(n, t)
                for t in range(NT):
                    modulate(n, t)
                for c in range(KC):
                    low(n, c)

            def slot(m, last):
                for i in range(NOUT):
                    if i < NQK:
                        dve.wait_ge(qk_act, NQK * m + i + 1)
                        r = i % RING
                        dve.tensor_tensor(out_lo[:, r, :], out_f[:, r, :], out_hi[:, r, :].bitcast(F32), ALU.subtract).then_inc(qk_lo, 1)
                    else:
                        t = i - NQK
                        dve.wait_ge(out_ps, NOUT * m + i + 1)
                        at_least(dve, v_out[t % 2], 16 * (NT // 2 * m + t // 2))
                        dve.tensor_tensor(v[:, t % 2, :], p_out[i % 3][:, :], bias_v[:, :], ALU.add).then_inc(v_set, 1)
                    if last:
                        continue
                    if i == 3:
                        cut_features(m + 1)
                    if 4 <= i < 4 + NT:
                        condition(m + 1, i - 4)
                    if i >= NQK:
                        modulate(m + 1, i - NQK)
                if not last:
                    for c in range(KC):
                        low(m + 1, c)

            slots(dve, front, slot)


def attention(nc, io, keep, scratch):
    with ExitStack() as ctx:
        k = Scope(nc, ctx, "b_")
        q = k.sb("q", [P, 2, HG, QP], F32R)
        key = k.sb("key", [P, HG, S], F32R)
        val = k.sb("val", [P, NKC, P])
        bias = k.sb("bias", [P, NBIAS, S])
        mask = k.sb("mask", [P, NQT, S], BF16)
        score = k.sb("score", [P, 2, S])
        prob = k.sb("prob", [P, 2, S])
        probt = k.sb("probt", [P, 2, HG, NKC, QP])
        negmax = k.sb("negmax", [P, 2, UQ])
        total = k.sb("total", [P, 2, UQ])
        recip = k.sb("recip", [P, 3, UQ])
        spread = k.sb("spread", [P, UQ, HD])
        recipt = k.sb("recipt", [P, QP])
        ctxn = k.sb("ctxn", [P, 2, QP])

        p_s = [k.ps(f"p_s{i}", [P, S]) for i in range(2)]
        p_ta, p_tb = k.ps("p_ta", [P, 512]), k.ps("p_tb", [P, 512])
        p_ctx = k.ps("p_ctx", [P, 512])
        p_rec = k.ps("p_rec", [P, 512])

        bias_in, q_in, key_in, mask_in = k.sems("bias_in", NBIAS), k.sems("q_in", 2), k.sems("key_in", HG), k.sems("mask_in", NQT)
        val_in, ctx_out = k.sem("val_in"), k.sems("ctx_out", 2)
        qk_ps, masked, score_set, prob_set, ta_ps, tb_ps, ta_set, tb_set = (
            k.sem(n) for n in ("qk_ps", "masked", "score_set", "prob_set", "ta_ps", "tb_ps", "ta_set", "tb_set"))
        recip_set, nan_set, spread_set, rec_ps, rec_set, ctx_ps, ctx_set = (
            k.sem(n) for n in ("recip_set", "nan_set", "spread_set", "rec_ps", "rec_set", "ctx_ps", "ctx_set"))
        ctx.callback(k.close)
        block = ctx.enter_context(nc.Block())

        NPH = len(POOL_HEADS)
        bias_u = io["fside_Bx16xSxS_0"].rearrange("b h (t p) k -> (b h) t p k", p=P)
        q_g = scratch["q"].rearrange("m (h r) s (u n) -> m u (r s) h n", h=HG, n=QP)
        key_g = scratch["k"].rearrange("m (h r) s n -> m h (r s) n", h=HG)
        ctx_g = scratch["ctx"]

        def at_half(g, half):
            return g + HG * (g // HG) + HG * half

        def unit(j):
            return j // UQ, j % UQ // 2, j % 2

        def masked_before(j):
            return sum(unit(i)[1] in POOL_HEADS for i in range(j))

        def groups(eng, group):
            group(0, True, False)
            with eng.Fori(1, NG - 1) as g:
                group(g, False, False)
            group(NG - 1, False, True)

        def ahead(g, j, last):
            if j < UG:
                return g, j
            return None if last else (g + 1, j - UG)

        @block.sync
        def _(sp):
            def group(g, masks):
                for j in range(UG):
                    u, h, t = unit(j)
                    if j % UQ == 0:
                        at_least(sp, qk_ps, UG * g + j - UQ)
                        sp.dma_start(q[:, u % 2, :, :].bitcast(F32), q_g[at_half(g, u // 2), u % 2]).then_inc(q_in[u % 2], 16)
                        if masks:
                            for i in range(2 * u, 2 * u + 2):
                                at_least(sp, score_set, UG * (g - 1) + UQ * (u + 1))
                                sp.dma_start(mask[:, i, :], scratch["mask"][NQT * (g // HG) + i]).then_inc(mask_in[i], 16)
                    if j < UQ and t == 0:
                        at_least(sp, qk_ps, UG * (g - 1) + UG - UQ + 2 * h + 2)
                        for half in range(2):
                            sp.dma_start(key[:, h, half * TB:(half + 1) * TB].bitcast(F32), key_g[at_half(g, half), h]).then_inc(key_in[h], 16)
                    if j == UQ + 5:
                        at_least(sp, ctx_ps, NQP * g)
                        for half in range(2):
                            sp.dma_start(val[:, half * NT:(half + 1) * NT, :], scratch["v"][at_half(g, half)]).then_inc(val_in, 16)
                    at_least(sp, score_set, UG * g + j - NBIAS + 1)
                    sp.dma_start(bias[:, j % NBIAS, :], bias_u[HG * g + h, 2 * u + t]).then_inc(bias_in[j % NBIAS], 16)

            group(0, True)
            with sp.Fori(1, HG) as g:
                group(g, False)
            with sp.Fori(1, B) as b:
                group(HG * b, True)
                with sp.Fori(1, HG) as i:
                    group(HG * b + i, False)

        @block.gpsimd
        def _(pool):
            def group(g, first, last):
                for j in range(UG):
                    u, h, t = unit(j)
                    if h not in POOL_HEADS:
                        continue
                    if j % UQ == 0:
                        pool.wait_ge(mask_in[2 * u], 16 * (g // HG + 1))
                        pool.wait_ge(mask_in[2 * u + 1], 16 * (g // HG + 1))
                    buf = j % NBIAS
                    pool.wait_ge(bias_in[buf], 16 * (UG // NBIAS * g + j // NBIAS + 1))
                    pool.tensor_tensor(bias[:, buf, :], bias[:, buf, :], mask[:, 2 * u + t, :], ALU.add).then_inc(masked, 1)

            with pool.Fori(0, NG) as g:
                group(g, False, False)

        @block.tensor
        def _(pe):
            def scores(g, j):
                u, h, t = unit(j)
                at_least(pe, score_set, UG * g + j - 1)
                if j % UQ == 0:
                    pe.wait_ge(q_in[u % 2], 16 * (NQP // 2 * g + u // 2 + 1))
                if j < UQ and t == 0:
                    pe.wait_ge(key_in[h], 32 * (g + 1))
                on_pe = h not in POOL_HEADS
                if on_pe:
                    pe.wait_ge(mask_in[2 * u + t], 16 * (g // HG + 1))
                for n in range(S // 512):
                    cols = slice(n * 512, (n + 1) * 512)
                    last = pe.matmul(p_s[j % 2][:, cols], q[:, u % 2, h, t * P:(t + 1) * P], key[:, h, cols], start=True, stop=not on_pe)
                    if on_pe:
                        last = pe.matmul(p_s[j % 2][:, cols], keep["identb"][:, :], mask[:, 2 * u + t, cols], start=False, stop=True)
                last.then_inc(qk_ps, 1)

            def transposes(g, j):
                s = UG * g + j
                pe.wait_ge(prob_set, s + 1)
                for half, (bank, taken, made) in enumerate(((p_ta, ta_set, ta_ps), (p_tb, tb_set, tb_ps))):
                    at_least(pe, taken, s)
                    for c in range(NKC // 2):
                        kc = half * (NKC // 2) + c
                        last = pe.transpose(bank[:, c * P:(c + 1) * P], prob[:, j % 2, kc * P:(kc + 1) * P], keep["ident"][:, :])
                    last.then_inc(made, 1)

            def values(g, u, kc):
                if kc == 0:
                    pairs = NQP * g + u
                    pe.wait_ge(ta_set, UQ * (pairs + 1))
                    pe.wait_ge(tb_set, UQ * (pairs + 1))
                    pe.wait_ge(val_in, 32 * (g + 1))
                    at_least(pe, ctx_set, pairs)
                for h in range(HG):
                    rows = slice(h * HD, (h + 1) * HD)
                    last = pe.matmul(p_ctx[rows, 0:QP], val[:, kc, rows], probt[:, u % 2, h, kc, :], start=kc == 0, stop=kc == NKC - 1)
                if kc == NKC - 1:
                    last.then_inc(ctx_ps, 1)

            def reciprocals(g, u):
                pairs = NQP * g + u
                pe.wait_ge(spread_set, pairs + 1)
                at_least(pe, rec_set, pairs)
                for t in range(2):
                    last = pe.transpose(p_rec[:, t * P:(t + 1) * P], spread[:, t * HG:(t + 1) * HG, :].rearrange("p h d -> p (h d)"),
                                        keep["ident"][:, :])
                last.then_inc(rec_ps, 1)

            def group(g, first, last):
                for j in range(UG):
                    u, r = j // UQ, j % UQ
                    then = ahead(g, j + 2, last)
                    if then:
                        scores(*then)
                    transposes(g, j)
                    if first and u == 0:
                        continue
                    of = (g, u - 1) if u else (g - 1, NQP - 1)
                    if r < NKC // 2:
                        values(*of, 2 * r)
                        values(*of, 2 * r + 1)
                    if r == 3:
                        reciprocals(*of)

            scores(0, 0)
            scores(0, 1)
            groups(pe, group)
            for kc in range(NKC):
                values(NG - 1, NQP - 1, kc)
            reciprocals(NG - 1, NQP - 1)

        @block.scalar
        def _(act):
            def exponentials(g, j):
                u, h, t = unit(j)
                s = UG * g + j
                act.wait_ge(score_set, s + 1)
                at_least(act, tb_ps, s - 1)
                if j % UQ == 0:
                    at_least(act, spread_set, NQP * g + u - 1)
                col = t * HG + h
                act.activation(prob[:, j % 2, :], score[:, j % 2, :], ACT.Exp, bias=negmax[:, u % 2, col:col + 1], scale=-1.0,
                               accum_out=total[:, u % 2, col:col + 1]).then_inc(prob_set, 1)

            def half_a(g, j):
                u, h, t = unit(j)
                act.wait_ge(ta_ps, UG * g + j + 1)
                if j % UQ == 0:
                    at_least(act, ctx_ps, NQP * g + u - 1)
                act.activation(probt[:, u % 2, h, 0:NKC // 2, t * P:(t + 1) * P], p_ta[:, :].rearrange("p (c n) -> p c n", n=P),
                               ACT.Copy).then_inc(ta_set, 1)

            def reciprocals(g, u):
                pairs = NQP * g + u
                act.wait_ge(rec_ps, pairs + 1)
                at_least(act, ctx_set, pairs)
                act.activation(recipt[:, :], p_rec[:, 0:QP], ACT.Copy).then_inc(rec_set, 1)

            def store(g, u):
                act.wait_ge(ctx_set, NQP * g + u + 1)
                act.dma_start(ctx_g[at_half(g, u // 2), :, (u % 2) * QP:(u % 2 + 1) * QP],
                              ctxn[:, u % 2, :]).then_inc(ctx_out[u % 2], 16)

            def group(g, first, last):
                for j in range(UG):
                    u, r = j // UQ, j % UQ
                    then = ahead(g, j + 1, last)
                    if then:
                        exponentials(*then)
                    half_a(g, j)
                    if first and u == 0:
                        continue
                    of = (g, u - 1) if u else (g - 1, NQP - 1)
                    if r == 4:
                        reciprocals(*of)
                    if r == 7:
                        store(*of)

            exponentials(0, 0)
            groups(act, group)
            reciprocals(NG - 1, NQP - 1)
            store(NG - 1, NQP - 1)
            for i in range(2):
                act.wait_ge(ctx_out[i], 16 * NG * NQP // 2)

        @block.vector
        def _(dve):
            def biased(g, j):
                u, h, t = unit(j)
                s = UG * g + j
                if h in POOL_HEADS:
                    addend, there = masked, counted(dve, masked_before(UG) * g + masked_before(j) + 1)
                else:
                    addend, there = bias_in[j % NBIAS], counted(dve, 16 * (UG // NBIAS * g + j // NBIAS + 1))
                scored, free = counted(dve, s + 1), counted(dve, s - 1)
                carried(dve, qk_ps)
                dve.wait_ge(qk_ps, scored)
                dve.wait_ge(addend, there)
                at_least(dve, prob_set, free)
                col = t * HG + h
                dve.tensor_tensor_reduce(score[:, j % 2, :], p_s[j % 2][:, :], bias[:, j % NBIAS, :], -1.0, HUGE,
                                         ALU.add, ALU.min, negmax[:, u % 2, col:col + 1]).then_inc(score_set, 1)

            def half_b(g, j):
                u, h, t = unit(j)
                dve.wait_ge(tb_ps, UG * g + j + 1)
                if j % UQ == 0:
                    at_least(dve, ctx_ps, NQP * g + u - 1)
                dve.tensor_copy(probt[:, u % 2, h, NKC // 2:NKC, t * P:(t + 1) * P],
                                p_tb[:, :].rearrange("p (c n) -> p c n", n=P)).then_inc(tb_set, 1)

            def reciprocals(g, u):
                pairs = NQP * g + u
                dve.wait_ge(prob_set, UQ * (pairs + 1))
                dve.reciprocal(recip[:, 0, :], total[:, u % 2, :]).then_inc(recip_set, 1)
                dve.tensor_scalar(recip[:, 1, :], negmax[:, u % 2, :], -0.1 * MASKED, HUGE, ALU.is_gt, ALU.mult).then_inc(nan_set, 1)
                dve.wait_ge(nan_set, 2 * pairs + 1)
                dve.tensor_scalar(recip[:, 2, :], recip[:, 1, :], HUGE, 0.0, ALU.mult, ALU.mult).then_inc(nan_set, 1)
                dve.wait_ge(nan_set, 2 * pairs + 2)
                dve.wait_ge(recip_set, pairs + 1)
                at_least(dve, rec_ps, pairs)
                dve.tensor_tensor(spread[:, :, :], recip[:, 0, :].unsqueeze(2).to_broadcast([P, UQ, HD]),
                                  recip[:, 2, :].unsqueeze(2).to_broadcast([P, UQ, HD]), ALU.add).then_inc(spread_set, 1)

            def normalize(g, u):
                pairs = NQP * g + u
                dve.wait_ge(ctx_ps, pairs + 1)
                dve.wait_ge(rec_set, pairs + 1)
                at_least(dve, ctx_out[u % 2], 16 * (NQP // 2 * g + u // 2))
                dve.tensor_tensor(ctxn[:, u % 2, :], p_ctx[:, 0:QP], recipt[:, :], ALU.mult).then_inc(ctx_set, 1)

            def group(g, first, last):
                for j in range(UG):
                    u, r = j // UQ, j % UQ
                    then = ahead(g, j + 1, last)
                    if then:
                        biased(*then)
                    half_b(g, j)
                    if first and u == 0:
                        continue
                    of = (g, u - 1) if u else (g - 1, NQP - 1)
                    if r == 1:
                        reciprocals(*of)
                    if r == 5:
                        normalize(*of)

            biased(0, 0)
            groups(dve, group)
            reciprocals(NG - 1, NQP - 1)
            normalize(NG - 1, NQP - 1)


def feed_forward(nc, io, keep, scratch, out):
    with ExitStack() as ctx:
        k = Scope(nc, ctx, "f_")
        wo = [k.sb(f"wo{i}", [P, KC, D], F32R) for i in range(2)]
        w1 = [k.sb(f"w1{i}", [P, KC, FF], F32R) for i in range(2)]
        w2 = [k.sb(f"w2{i}", [P, FC, D], F32R) for i in range(2)]
        raw = k.sb("raw", [P, 2, D])
        cx = k.sb("cx", [P, KC, P])
        cx_hi = k.sb("cx_hi", [P, 2, KC, P], F32R)
        cx_lo = k.sb("cx_lo", [P, 2, KC, P], F32R)
        y = k.sb("y", [P, NT, D])
        yb = k.sb("yb", [P, D])
        stats = k.sb("stats", [P, NT, 6])
        meanvar = k.sb("meanvar", [P, NT, 2])
        rstd = k.sb("rstd", [P, NT, 2])
        ht_f = k.sb("ht_f", [P, TB])
        ht_hi = k.sb("ht_hi", [P, KC, TB], F32R)
        ht_lo = k.sb("ht_lo", [P, KC, TB], F32R)
        act_f = k.sb("act_f", [P, 2, TB])
        act_hi = k.sb("act_hi", [P, 2, TB], F32R)
        act_lo = k.sb("act_lo", [P, 2, TB], F32R)
        o = k.sb("o", [P, 2, D])
        g2 = k.sb("g2", [P, KC])
        beta2 = k.sb("beta2", [P, KC])
        b1 = k.sb("b1", [P, 2, FC])
        b2 = k.sb("b2", [P, D])

        p_h = [k.ps(f"p_h{i}", [P, 512]) for i in range(2)]
        p_o = [k.ps(f"p_o{i}", [P, 512]) for i in range(NT)]
        p_f = [k.ps(f"p_f{i}", [P, 512]) for i in range(2)]

        raw_in, small_in, cx_in, y_in, yb_out, yb_in, o_out = (
            k.sems("raw_in", 2), k.sem("small_in"), k.sem("cx_in"), k.sem("y_in"), k.sem("yb_out"), k.sems("yb_in", 2), k.sems("o_out", 2))
        w_hi, w_lo, b1_set, cx_hi_set, cx_set, proj_ps, y_set, bn_set, stats_set, eps_set, rstd_set = (
            k.sem(n) for n in ("w_hi", "w_lo", "b1_set", "cx_hi_set", "cx_set", "proj_ps", "y_set", "bn_set", "stats_set", "eps_set", "rstd_set"))
        yb_set, ln_set, t_ps, htf_set, hi_set, lo_set, up_ps, sig_set, act_set, act_hi_set, act_lo_set, down_ps, out_ps, o_set = (
            k.sem(n) for n in ("yb_set", "ln_set", "t_ps", "htf_set", "hi_set", "lo_set", "up_ps", "sig_set", "act_set", "act_hi_set",
                               "act_lo_set", "down_ps", "out_ps", "o_set"))
        ctx.callback(k.close)
        block = ctx.enter_context(nc.Block())

        wo_v = io["L1_cond_Wo"].rearrange("(c p) n -> c p n", p=P)
        w1_v = io["L1_cond_W1"].rearrange("(c p) (g n) -> g c p n", p=P, n=D)
        w2_v = io["L1_cond_W2"].rearrange("(f p) n -> f p n", p=P)
        pieces = [(wo_v[c], wo, (c, slice(0, D))) for c in range(KC)]
        pieces += [(w1_v[0, c], w1, (c, slice(0, D))) for c in range(KC)]
        FIRST = len(pieces)
        due = []
        for f in range(FC):
            pieces.append((w2_v[f], w2, (f, slice(0, D))))
            g = f // KC + 1
            if g < FF // D:
                pieces.append((w1_v[g, f % KC], w1, (f % KC, slice(g * D, (g + 1) * D))))
            due.append(len(pieces))

        def due_w1(f):
            return FIRST if f < KC else due[KC * (f // KC) - 1]

        xo_blk = scratch["xo"].rearrange("(n t p) d -> n p t d", t=NT, p=P)
        yb_blk = scratch["yb"].rearrange("(n t p) d -> n t p d", t=NT, p=P)
        out_blk = out.rearrange("b (n t p) d -> (b n) t p d", t=NT, p=P)
        ctx_blk = scratch["ctx"].rearrange("(n c) p (t q) -> n t p c q", c=KC, t=NT)

        def slots(eng, front, slot):
            front(0)
            slot(0, False)
            with eng.Fori(1, NBLK - 1) as m:
                slot(m, False)
            slot(NBLK - 1, True)

        @block.sync
        def _(sp):
            sp.dma_start(b1[:, 0, :], io["L1_cond_b1"].rearrange("(f p) -> p f", p=P)).then_inc(small_in, 16)
            sp.dma_start(g2[:, :], io["L1_cond_g2"].rearrange("(c p) -> p c", p=P)).then_inc(small_in, 16)
            sp.dma_start(beta2[:, :], io["L1_cond_beta2"].rearrange("(c p) -> p c", p=P)).then_inc(small_in, 16)
            sp.dma_start(b2[:, :], io["L1_cond_b2"].partition_broadcast(P)).then_inc(small_in, 16)

            def load_y(n):
                at_least(sp, t_ps, KC * n)
                sp.dma_start(y[:, :, :], xo_blk[n]).then_inc(y_in, 16)

            def load_cx(n, t):
                at_least(sp, cx_set, NT * n + t)
                sp.dma_start(cx[:, :, :], ctx_blk[n, t]).then_inc(cx_in, 16)

            def store_yb(n, t):
                sp.wait_ge(yb_set, NT * n + t + 1)
                sp.dma_start(yb_blk[n, t], yb[:, :]).then_inc(yb_out, 16)

            def load_yb(m, t):
                sp.wait_ge(yb_out, 16 * (NT * m + t + 1))
                at_least(sp, o_out[t % 2], 16 * (NT // 2 * m + t // 2))
                sp.dma_start(o[:, t % 2, :], yb_blk[m, t]).then_inc(yb_in[t % 2], 16)

            def store_o(m, t):
                sp.wait_ge(o_set, NT * m + t + 1)
                sp.dma_start(out_blk[m, t], o[:, t % 2, :]).then_inc(o_out[t % 2], 16)

            def front(n):
                load_y(n)
                for t in range(NT):
                    load_cx(n, t)
                    if t >= 2:
                        store_yb(n, t - 2)
                for t in range(NT - 2, NT):
                    store_yb(n, t)

            def outputs(m):
                load_yb(m, 0)
                load_yb(m, 1)
                for t in range(NT):
                    store_o(m, t)
                    if t + 2 < NT:
                        load_yb(m, t + 2)

            def load_pieces(first, end):
                for n in range(first, end):
                    at_least(sp, w_lo, n - 1)
                    sp.dma_start(raw[:, n % 2, :], pieces[n][0]).then_inc(raw_in[n % 2], 16)

            load_y(0)
            load_pieces(0, FIRST)
            for t in range(NT):
                load_cx(0, t)
                if t >= 2:
                    store_yb(0, t - 2)
            for t in range(NT - 2, NT):
                store_yb(0, t)
            for f in range(FC):
                load_pieces(due[f - 1] if f else FIRST, due[f])
                if f == 0:
                    load_y(1)
                if f in (0, 2, 4, 6):
                    load_cx(1, f // 2)
                if f in (4, 6, 8, 10):
                    store_yb(1, f // 2 - 2)
            outputs(0)
            with sp.Fori(1, NBLK - 1) as m:
                front(m + 1)
                outputs(m)
            outputs(NBLK - 1)
            for i in range(2):
                sp.wait_ge(o_out[i], 16 * NBLK * NT // 2)

        @block.gpsimd
        def _(pool):
            pool.wait_ge(small_in, 64)

            def front(n):
                for t in range(NT):
                    tile = NT * n + t + 1
                    pool.wait_ge(y_set, tile)
                    at_least(pool, yb_out, 16 * (tile - 1))
                    pool.tensor_tensor(yb[:, :], y[:, t, :], b2[:, :], ALU.add).then_inc(yb_set, 1)
                    pool.wait_ge(stats_set, tile)
                    pool.tensor_tensor(rstd[:, t, 0:1], meanvar[:, t, 1:2], keep["eps"][:, :], ALU.add).then_inc(eps_set, 1)
                    pool.wait_ge(eps_set, tile)
                    pool.tensor_tensor(rstd[:, t, 1:2], rstd[:, t, 0:1], keep["neghalf"][:, :], ALU.pow).then_inc(rstd_set, 1)

            front(0)
            with pool.Fori(1, NBLK) as n:
                front(n)

        @block.tensor
        def _(pe):
            def project(n, t):
                if t == 0:
                    at_least(pe, w_lo, KC) if isinstance(n, int) else None
                pe.wait_ge(cx_set, NT * n + t + 1)
                if t < 2:
                    at_least(pe, lo_set, KC * n - 1 + t)
                else:
                    pe.wait_ge(y_set, NT * n + t - 1)
                products = []
                for c in range(KC):
                    hi, lo = cx_hi[:, t % 2, c, :], cx_lo[:, t % 2, c, :]
                    products += [(hi, wo[0][:, c, :]), (hi, wo[1][:, c, :]), (lo, wo[0][:, c, :])]
                for i, (left, right) in enumerate(products):
                    last = pe.matmul(p_f[t % 2][:, :], left, right, start=i == 0, stop=i == len(products) - 1)
                last.then_inc(proj_ps, 1)

            def transpose(n, c):
                if c == 0:
                    pe.wait_ge(ln_set, NT * (n + 1))
                if c >= 2:
                    pe.wait_ge(lo_set, KC * n + c - 1)
                for t in range(NT):
                    last = pe.transpose(p_f[c % 2][:, t * P:(t + 1) * P], y[:, t, c * P:(c + 1) * P], keep["ident"][:, :])
                last.then_inc(t_ps, 1)

            def up(m, f):
                if f == 0:
                    pe.wait_ge(lo_set, KC * (m + 1))
                at_least(pe, act_set, FC * m + f - 1)
                cols = slice(f * P, (f + 1) * P)
                if isinstance(m, int) and m == 0:
                    pe.wait_ge(w_lo, due_w1(f))
                products = []
                for c in range(KC):
                    hi, lo = w1[0][:, c, cols], w1[1][:, c, cols]
                    products += [(hi, ht_hi[:, c, :]), (hi, ht_lo[:, c, :]), (lo, ht_hi[:, c, :])]
                for i, (left, right) in enumerate(products):
                    last = pe.matmul(p_h[f % 2][:, :], left, right, start=i == 0, stop=i == len(products) - 1)
                last.then_inc(up_ps, 1)

            def down(m, f):
                pe.wait_ge(act_lo_set, FC * m + f + 1)
                pe.wait_ge(act_hi_set, FC * m + f + 1)
                if isinstance(m, int) and m == 0:
                    pe.wait_ge(w_lo, due[f])
                for t in range(NT):
                    if f == 0:
                        at_least(pe, o_set, NT * (m - 1) + t + 1)
                    cols = slice(t * P, (t + 1) * P)
                    hi, lo = act_hi[:, f % 2, cols], act_lo[:, f % 2, cols]
                    pe.matmul(p_o[t][:, :], hi, w2[0][:, f, :], start=f == 0, stop=False)
                    pe.matmul(p_o[t][:, :], hi, w2[1][:, f, :], start=False, stop=False)
                    last = pe.matmul(p_o[t][:, :], lo, w2[0][:, f, :], start=False, stop=f == FC - 1)
                    if f == FC - 1:
                        last.then_inc(out_ps, 1)
                if f < FC - 1:
                    last.then_inc(down_ps, 1)

            def front(n):
                for t in range(NT):
                    project(n, t)
                for c in range(KC):
                    transpose(n, c)

            def slot(m, last):
                up(m, 0)
                up(m, 1)
                for f in range(FC):
                    if f + 2 < FC:
                        up(m, f + 2)
                    down(m, f)
                    if last:
                        continue
                    if f in (1, 3, 5, 7):
                        project(m + 1, (f - 1) // 2)
                    if f == FC - 3:
                        transpose(m + 1, 0)
                        transpose(m + 1, 1)
                    if f == FC - 2:
                        transpose(m + 1, 2)
                        transpose(m + 1, 3)

            slots(pe, front, slot)

        @block.scalar
        def _(act):
            act.wait_ge(small_in, 64)
            act.activation(b1[:, 1, :], b1[:, 0, :], ACT.Copy, scale=1.702).then_inc(b1_set, 1)
            act.wait_ge(b1_set, 1)

            def cut(first, end):
                for n in range(first, end):
                    act.wait_ge(raw_in[n % 2], 16 * (n // 2 + 1))
                    _, w, at = pieces[n]
                    act.activation(w[0][:, at[0], at[1]], raw[:, n % 2, :], ACT.Copy).then_inc(w_hi, 1)

            def high_cx(n, t):
                tile = NT * n + t
                act.wait_ge(cx_in, 16 * (tile + 1))
                at_least(act, proj_ps, tile - 1)
                act.activation(cx_hi[:, t % 2, :, :], cx[:, :, :], ACT.Copy).then_inc(cx_hi_set, 1)

            def normed(n, c):
                act.wait_ge(t_ps, KC * n + c + 1)
                at_least(act, up_ps, FC * n)
                at_least(act, lo_set, KC * n + c)
                act.activation(ht_f[:, :], p_f[c % 2][:, :], ACT.Identity, scale=g2[:, c:c + 1], bias=beta2[:, c:c + 1]).then_inc(htf_set, 1)
                act.activation(ht_hi[:, c, :], p_f[c % 2][:, :], ACT.Identity, scale=g2[:, c:c + 1], bias=beta2[:, c:c + 1]).then_inc(hi_set, 1)

            def front(n):
                cut(0, FIRST)
                for t in range(NT):
                    high_cx(n, t)
                for c in range(KC):
                    normed(n, c)

            def slot(m, last):
                for f in range(FC):
                    if isinstance(m, int) and m == 0:
                        cut(due[f - 1] if f else FIRST, due[f])
                    i = FC * m + f
                    act.wait_ge(up_ps, i + 1)
                    at_least(act, act_lo_set, i - 1)
                    at_least(act, act_hi_set, i - 1)
                    act.activation(act_f[:, f % 2, :], p_h[f % 2][:, :], ACT.Sigmoid, scale=1.702, bias=b1[:, 1, f:f + 1]).then_inc(sig_set, 1)
                    if last:
                        continue
                    if f in (0, 2, 4, 6):
                        high_cx(m + 1, f // 2)
                    if f == FC - 2:
                        normed(m + 1, 0)
                        normed(m + 1, 1)
                    if f == FC - 1:
                        normed(m + 1, 2)
                        normed(m + 1, 3)

            slots(act, front, slot)

        @block.vector
        def _(dve):
            dve.wait_ge(small_in, 64)

            def cut(first, end):
                for n in range(first, end):
                    dve.wait_ge(w_hi, n + 1)
                    _, w, at = pieces[n]
                    dve.tensor_tensor(w[1][:, at[0], at[1]], raw[:, n % 2, :], w[0][:, at[0], at[1]].bitcast(F32), ALU.subtract).then_inc(w_lo, 1)

            def low_cx(n, t):
                dve.wait_ge(cx_hi_set, NT * n + t + 1)
                dve.tensor_tensor(cx_lo[:, t % 2, :, :], cx[:, :, :], cx_hi[:, t % 2, :, :].bitcast(F32), ALU.subtract).then_inc(cx_set, 1)

            def attended(n, t):
                tile = NT * n + t + 1
                dve.wait_ge(proj_ps, tile)
                dve.wait_ge(y_in, 16 * (n + 1))
                dve.tensor_tensor(y[:, t, :], p_f[t % 2][:, :], y[:, t, :], ALU.add).then_inc(y_set, 1)
                dve.wait_ge(y_set, tile)
                dve.bn_stats(stats[:, t, :], y[:, t, :]).then_inc(bn_set, 1)
                carried(dve, bn_set)
                dve.wait_ge(bn_set, tile)
                dve.bn_aggr(meanvar[:, t, :], stats[:, t, :]).then_inc(stats_set, 1)

            def normalize(n, t):
                tile = NT * n + t + 1
                dve.wait_ge(rstd_set, tile)
                dve.wait_ge(stats_set, tile)
                dve.wait_ge(yb_set, tile)
                dve.tensor_scalar(y[:, t, :], y[:, t, :], meanvar[:, t, 0:1], rstd[:, t, 1:2], ALU.subtract, ALU.mult).then_inc(ln_set, 1)

            def low(n, c):
                dve.wait_ge(hi_set, KC * n + c + 1)
                dve.wait_ge(htf_set, KC * n + c + 1)
                dve.tensor_tensor(ht_lo[:, c, :], ht_f[:, :], ht_hi[:, c, :].bitcast(F32), ALU.subtract).then_inc(lo_set, 1)

            def front(n):
                cut(0, FIRST)
                for t in range(NT):
                    low_cx(n, t)
                    if t:
                        attended(n, t - 1)
                attended(n, NT - 1)
                for t in range(NT):
                    normalize(n, t)
                for c in range(KC):
                    low(n, c)

            def slot(m, last):
                for f in range(FC):
                    if isinstance(m, int) and m == 0:
                        cut(due[f - 1] if f else FIRST, due[f])
                    i = FC * m + f
                    b = f % 2
                    dve.wait_ge(sig_set, i + 1)
                    dve.scalar_tensor_tensor(act_f[:, b, :], p_h[b][:, :], b1[:, 0, f:f + 1], act_f[:, b, :], ALU.add, ALU.mult).then_inc(act_set, 1)
                    dve.wait_ge(act_set, i + 1)
                    if f < 2:
                        at_least(dve, out_ps, NT * m)
                        at_least(dve, down_ps, (FC - 1) * m)
                    else:
                        dve.wait_ge(down_ps, (FC - 1) * m + f - 1)
                    dve.tensor_copy(act_hi[:, b, :], act_f[:, b, :]).then_inc(act_hi_set, 1)
                    dve.wait_ge(act_hi_set, i + 1)
                    dve.tensor_tensor(act_lo[:, b, :], act_f[:, b, :], act_hi[:, b, :].bitcast(F32), ALU.subtract).then_inc(act_lo_set, 1)
                    if not last:
                        if f in (0, 2, 4, 6):
                            low_cx(m + 1, f // 2)
                        if f in (2, 4, 6, 8):
                            attended(m + 1, f // 2 - 1)
                        if f == 10:
                            for t in range(NT):
                                normalize(m + 1, t)
                        if f == FC - 2:
                            low(m + 1, 0)
                            low(m + 1, 1)
                for t in range(NT):
                    dve.wait_ge(out_ps, NT * m + t + 1)
                    dve.wait_ge(yb_in[t % 2], 16 * (NT // 2 * m + t // 2 + 1))
                    dve.tensor_tensor(o[:, t % 2, :], p_o[t][:, :], o[:, t % 2, :], ALU.add).then_inc(o_set, 1)
                    if t < 2 and not last:
                        low(m + 1, 2 + t)

            slots(dve, front, slot)


def build(nc, io, out):
    with nc.allow_non_contiguous_dma(reason="bias columns of a few hundred elements"):
        build_stages(nc, io, out)


def build_stages(nc, io, out):
    scratch = {
        "cond": nc.dram_tensor("cond_scratch", (B, P, CW), F32).ap(),
        "q": nc.dram_tensor("q_scratch", (NBLK * KC, P, 4, TB), F32).ap(),
        "k": nc.dram_tensor("k_scratch", (NBLK * KC, P, 4, TB), F32).ap(),
        "v": nc.dram_tensor("v_scratch", (NBLK * KC, P, NT, P), F32).ap(),
        "mask": nc.dram_tensor("mask_scratch", (B * NQT, P, S), BF16).ap(),
        "xo": nc.dram_tensor("xo_scratch", (B * S, D), F32).ap(),
        "ctx": nc.dram_tensor("ctx_scratch", (NBLK * KC, P, TB), F32).ap(),
        "yb": nc.dram_tensor("yb_scratch", (B * S, D), F32).ap(),
    }
    with ExitStack() as ctx:
        k = Scope(nc, ctx, "k_")
        keep = {"ident": k.sb("ident", [P, P]), "identb": k.sb("identb", [P, P], BF16), "neghalf": k.sb("neghalf", [P, 1]), "eps": k.sb("eps", [P, 1])}
        with ExitStack() as early:
            e = Scope(nc, early, "e_")
            keep["m4"] = e.sb("m4", [P, KC, P])
            keep["rw"] = e.sb("rw", [P, D], F32R)
            keep["wqkv"] = [tuple(e.sb(f"w{n}{part}", [P, KC, D], F32R) for part in ("hi", "lo")) for n in "qkv"]
            conditioning(nc, io, keep, scratch)
            projections(nc, io, keep, scratch)
        attention(nc, io, keep, scratch)
        feed_forward(nc, io, keep, scratch, out)


def frequencies():
    half = D // 2
    freqs = np.exp(np.arange(half, dtype=np.float32) * np.float32(-math.log(10000.0) / (half - 1)))
    return np.ascontiguousarray(freqs.astype(np.float32).reshape(2, P).T)


def kernel(**inputs):
    import concourse.bacc as bacc
    from concourse.bass_utils import run_bass_kernel_spmd

    nc = bacc.Bacc("TRN2", target_bir_lowering=False, num_devices=1)
    arrays, io = {}, {}
    for name, value in [*inputs.items(), ("freq", frequencies())]:
        a = np.ascontiguousarray(value)
        arrays[f"in_{name}"] = a
        io[name] = nc.dram_tensor(f"in_{name}", a.shape, mybir.dt.from_np(a.dtype), kind="ExternalInput").ap()
    out = nc.dram_tensor("out", (B, S, D), F32, kind="ExternalOutput").ap()
    build(nc, io, out)
    result = run_bass_kernel_spmd(nc, [arrays], core_ids=[0])
    return result.results[0]["out"]
```

```python
import math
from contextlib import ExitStack

import numpy as np

import concourse.bass as bass
from concourse import mybir

F32 = mybir.dt.float32
F32R = mybir.dt.float32r
BF16 = mybir.dt.bfloat16
I32 = mybir.dt.int32
U8 = mybir.dt.uint8
ALU = mybir.AluOpType
ACT = mybir.ActivationFunctionType

P = 128
B, S, D, H = 4, 1024, 512, 16
HD = D // H
R = 32
FF = 2048
KC = D // P
FC = FF // P
TB = 512
NT = TB // P
NBLK = B * S // TB
HG = 4
NG = B * H // HG
NQT = S // P
NKC = S // P
QP = 2 * P
NQP = S // QP
UQ = HG * QP // P
UG = NQP * UQ
NBIAS = 16
NPROB = 4
SCORES_AHEAD = 3
BIASED_AHEAD = 3
EXP_AHEAD = 2
PE_MASKS = (3,)
ACT_BOTH = (3,)
MASKED = -1.0e30
HUGE = 3.0e38
LN_EPS = 1e-5
CW = 3 * D + 4
RING = 4

ROUND = 12582912.0
TWO_PI = (6.28125, 0.0019340515136718750, float(2 * math.pi - 6.28125 - 0.0019340515136718750))
PI_MAX = 3.1415925


def at_least(eng, sem, value):
    if isinstance(value, int) and value <= 0:
        return
    eng.wait_ge(sem, value)


def carried(eng, sem):
    eng.wait_ge(sem, 1)


def counted(eng, value):
    return value if isinstance(value, int) else eng.to_reg(value)


def chain_on(eng, sem):
    count = [0]

    def link(ins):
        count[0] += 1
        ins.then_inc(sem, 1)
        eng.wait_ge(sem, count[0])
        return ins

    return link


class Scope:

    def __init__(self, nc, ctx, prefix):
        self.nc, self.ctx, self.prefix, self.taken = nc, ctx, prefix, []

    def sb(self, name, shape, dt=F32):
        return self.ctx.enter_context(self.nc.sbuf_tensor(self.prefix + name, shape, dt))

    def ps(self, name, shape):
        return self.ctx.enter_context(self.nc.psum_tensor(self.prefix + name, shape, F32))

    def sem(self, name):
        self.taken.append(self.nc.alloc_semaphore(self.prefix + name))
        return self.taken[-1]

    def sems(self, name, n):
        return [self.sem(f"{name}{i}") for i in range(n)]

    def close(self):
        self.nc.clear_and_free_semaphores(self.taken)
        self.nc.all_engine_barrier()


def conditioning(nc, io, keep, scratch):
    with ExitStack() as ctx:
        k = Scope(nc, ctx, "c_")
        uv = k.sb("uv", [P, KC, 2 * R])
        uvt = k.sb("uvt", [2 * R, D])
        row = k.sb("row", [2 * R, D])
        sq_junk = k.sb("sq_junk", [2 * R, D])
        dot_junk = k.sb("dot_junk", [2 * R, D])
        norm2 = k.sb("norm2", [2 * R, 1])
        norm = k.sb("norm", [2 * R, 1])
        dot = k.sb("dot", [2 * R, 1])
        normeps = k.sb("normeps", [2 * R, 1])
        coef = k.sb("coef", [2 * R, 2])
        inv = k.sb("inv", [2 * R, R])
        own = k.sb("own", [2 * R, 1])
        eye = k.sb("eye", [2 * R, R])
        later = k.sb("later", [2 * R, R])
        basis = k.sb("basis", [P, KC, 2 * R])
        vtv = k.sb("vtv", [R, R])
        core4 = k.sb("core4", [R, P])
        rw = k.sb("rw", [P, KC, R])
        rw4 = k.sb("rw4", [P, KC, 4 * R])
        w1 = k.sb("w1", [P, D])
        w1t = k.sb("w1t", [P, KC, P])
        wada = k.sb("wada", [P, KC, 2 * D])
        bada = k.sb("bada", [P, 2 * D])
        xin = k.sb("xin", [P, 2, NQT, D])
        sums = k.sb("sums", [1, B, D])
        pooled = k.sb("pooled", [P, KC * B])
        hid = k.sb("hid", [P, B])
        gw2 = k.sb("gw2", [P, 1])
        gb1 = k.sb("gb1", [P, 1])
        gb2 = k.sb("gb2", [P, 1])
        safety = k.sb("safety", [P, B])
        gate = k.sb("gate", [P, 2, B])
        cond = k.sb("cond", [P, B, CW])
        rbias = k.sb("rbias", [P, 2, D])
        tok = k.sb("tok", [P, B], I32)
        tokf = k.sb("tokf", [P, 2, B])
        freq = k.sb("freq", [P, 2])
        angle = k.sb("angle", [P, 2, B])
        turns = k.sb("turns", [P, 4, B])
        arg = k.sb("arg", [P, 4, B])
        emb = k.sb("emb", [P, 4, B])
        ones = k.sb("ones", [P, 1])
        wraw = k.sb("wraw", [P, D * 2])

        p_uv = k.ps("p_uv", [P, 512])
        p_ada = [k.ps(f"p_ada{i}", [P, 512]) for i in range(2)]
        p_sum = [k.ps(f"p_sum{i}", [P, 512]) for i in range(2)]
        p_w1 = k.ps("p_w1", [P, 512])
        p_rw = k.ps("p_rw", [P, 512])
        p_small = k.ps("p_small", [P, 512])

        uv_in, rw_in, tok_in, freq_in, ada_in, bada_in = (k.sem(n) for n in ("uv_in", "rw_in", "tok_in", "freq_in", "ada_in", "bada_in"))
        w1_in, gate_in, rb_in, wraw_in = (k.sem(n) for n in ("w1_in", "gate_in", "rb_in", "wraw_in"))
        x_in = k.sems("x_in", 2)
        ident_set, eye_set, later_set, ones_set, rw4_set = (k.sem(n) for n in ("ident_set", "eye_set", "later_set", "ones_set", "rw4_set"))
        uvt_ps, uvt_set, row_set, norm_set = (k.sem(n) for n in ("uvt_ps", "uvt_set", "row_set", "norm_set"))
        arg_set, emb_set, ada_ps, ada_out, ada_added = (k.sem(n) for n in ("arg_set", "emb_set", "ada_ps", "ada_out", "ada_added"))
        w1t_ps, w1t_set, rw_ps, rw_hi, sum_ps, sum_set = (k.sem(n) for n in ("w1t_ps", "w1t_set", "rw_ps", "rw_hi", "sum_ps", "sum_set"))
        pooled_ps, pooled_set, hid_ps, hid_set, gate_ps, gate_set = (k.sem(n) for n in ("pooled_ps", "pooled_set", "hid_ps", "hid_set", "gate_ps", "gate_set"))
        ortho, basis_ps, basis_set, vtv_ps, vtv_set, core_ps, core_set, m_ps = (
            k.sem(n) for n in ("ortho", "basis_ps", "basis_set", "vtv_ps", "vtv_set", "core_ps", "core_set", "m_ps"))
        rb_set, done, stored, split_done = (k.sem(n) for n in ("rb_set", "done", "stored", "split_done"))
        dot_set, later_dot = k.sem("dot_set"), k.sem("later_dot")
        dve_own, act_own, pool_own = (k.sem(n) for n in ("dve_own", "act_own", "pool_own"))

        ctx.callback(k.close)
        block = ctx.enter_context(nc.Block())
        splits = [(src, c0) for src in range(3) for c0 in range(0, KC, 2)]

        @block.sync
        def _(sp):
            for half, w in enumerate((io["L0_cond_U"], io["L0_cond_V"])):
                sp.dma_start(uv[:, :, half * R:(half + 1) * R], w.rearrange("(c p) r -> p c r", p=P)).then_inc(uv_in, 16)
            sp.dma_start(tok[:, :], io["itok_B_34_63"].partition_broadcast(P)).then_inc(tok_in, 16)
            sp.dma_start(freq[:, :], io["freq"]).then_inc(freq_in, 16)
            sp.dma_start(wada[:, :, :], io["L1_cond_W_ada"].rearrange("(c p) n -> p c n", p=P)).then_inc(ada_in, 16)
            sp.dma_start(bada[:, :], io["L1_cond_b_ada"].partition_broadcast(P)).then_inc(bada_in, 16)
            sp.dma_start(rw[:, :, :], io["L0_cond_resp_w"].rearrange("(c p) r -> p c r", p=P)).then_inc(rw_in, 16)
            sp.dma_start(w1[:, :], io["L0_cond_gate_w1"]).then_inc(w1_in, 16)
            sp.dma_start(gw2[:, :], io["L0_cond_gate_w2"].rearrange("o p -> p o")).then_inc(gate_in, 16)
            sp.dma_start(gb1[:, :], io["L0_cond_gate_b1"].rearrange("(p o) -> p o", o=1)).then_inc(gate_in, 16)
            sp.dma_start(gb2[:, :], io["L0_cond_gate_b2"].partition_broadcast(P)).then_inc(gate_in, 16)
            sp.dma_start(safety[:, :], io["condB_safetyscore"].partition_broadcast(P)).then_inc(gate_in, 16)
            sp.dma_start(rbias[:, 0, :], io["L0_cond_resp_b"].partition_broadcast(P)).then_inc(rb_in, 16)
            sp.dma_start(rbias[:, 1, :], io["L0_cond_safety_bias"].partition_broadcast(P)).then_inc(rb_in, 16)
            for b in range(B):
                if b >= 2:
                    sp.wait_ge(sum_ps, b - 1)
                sp.dma_start(xin[:, b % 2], io["x"][b].rearrange("(t p) d -> p t d", p=P)).then_inc(x_in[b % 2], 16)
            for n, (src, c0) in enumerate(splits):
                w = (io["L1_cond_Wq"], io["L1_cond_Wk"], io["L1_cond_Wv"])[src]
                if n:
                    sp.wait_ge(split_done, n)
                sp.dma_start(wraw[:, :].rearrange("p (c n) -> p c n", c=2),
                             w.rearrange("(c p) n -> p c n", p=P)[:, c0:c0 + 2, :]).then_inc(wraw_in, 16)
            sp.wait_ge(ada_added, 2 * B)
            sp.wait_ge(done, B)
            sp.dma_start(scratch["cond"].rearrange("(o b) n -> o b n", o=1), cond[0:1, :, :]).then_inc(stored, 16)
            sp.wait_ge(stored, 16)

        @block.gpsimd
        def _(pool):
            link = chain_on(pool, pool_own)
            ident = keep["ident"]
            link(pool.memset(ident[:, :], 0.0))
            pool.affine_select(out=ident[:, :], in_=ident[:, :], compare_op=ALU.not_equal, fill=1.0,
                               base=0, pattern=[[-1, P]], channel_multiplier=1).then_inc(ident_set, 1)
            link(pool.memset(eye[:, :], 0.0))
            link(pool.memset(later[:, :], -1.0))
            for q in range(2):
                pool.affine_select(out=eye[q * R:(q + 1) * R, :], in_=eye[q * R:(q + 1) * R, :], compare_op=ALU.not_equal,
                                   fill=1.0, base=0, pattern=[[-1, R]], channel_multiplier=1).then_inc(eye_set, 1)
                pool.wait_ge(eye_set, q + 1)
                pool.affine_select(out=later[q * R:(q + 1) * R, :], in_=later[q * R:(q + 1) * R, :], compare_op=ALU.is_gt,
                                   fill=0.0, base=0, pattern=[[-1, R]], channel_multiplier=1).then_inc(later_set, 1)
                pool.wait_ge(later_set, q + 1)
            link(pool.memset(ones[:, :], 1.0))
            link(pool.memset(keep["neghalf"][:, :], -0.5))
            link(pool.memset(keep["eps"][:, :], LN_EPS))
            link(pool.memset(cond[:, :, 3 * D:CW], 0.0))
            pool.wait_ge(ident_set, 1)
            pool.tensor_copy(keep["identb"][:, :], ident[:, :]).then_inc(ones_set, 1)
            pool.wait_ge(ones_set, 1)
            pool.wait_ge(rw_in, 16)
            for q in range(4):
                pool.tensor_copy(rw4[:, :, q * R:(q + 1) * R], rw[:, :, :]).then_inc(rw4_set, 1)
                pool.wait_ge(rw4_set, q + 1)
            pool.wait_ge(bada_in, 16)
            link(pool.tensor_scalar(bada[:, 0:D], bada[:, 0:D], 1.0, None, ALU.add))
            pool.wait_ge(rb_in, 32)
            pool.tensor_tensor(rbias[:, 0, :], rbias[:, 0, :], rbias[:, 1, :], ALU.add).then_inc(rb_set, 1)
            for n in range(2 * B):
                b, half = divmod(n, 2)
                pool.wait_ge(ada_out, n + 1)
                part = cond[:, b, half * D:(half + 1) * D]
                pool.tensor_tensor(part, part, bada[:, half * D:(half + 1) * D], ALU.add).then_inc(ada_added, 1)
            for n, (src, c0) in enumerate(splits):
                pool.wait_ge(wraw_in, 16 * (n + 1))
                hi, lo = keep["wqkv"][src]
                raw = wraw[:, :].rearrange("p (c n) -> p c n", c=2)
                link(pool.tensor_copy(hi[:, c0:c0 + 2, :], raw))
                pool.tensor_tensor(lo[:, c0:c0 + 2, :], raw, hi[:, c0:c0 + 2, :].bitcast(F32), ALU.subtract).then_inc(split_done, 1)
            pool.wait_ge(gate_set, 2)
            link(pool.tensor_tensor(cond[:, :, 3 * D:3 * D + 1], gate[:, 0, :].unsqueeze(2), gate[:, 1, :].unsqueeze(2), ALU.mult))
            pool.wait_ge(rb_set, 1)
            for b in range(B):
                pool.tensor_tensor(cond[0:1, b, 2 * D:3 * D], rbias[0:1, 0, :], cond[0:1, b, 3 * D:3 * D + 1].to_broadcast([1, D]),
                                   ALU.mult).then_inc(done, 1)

        @block.tensor
        def _(pe):
            ident = keep["ident"][:, :]
            pe.wait_ge(ident_set, 1)
            pe.wait_ge(uv_in, 32)
            for c in range(KC):
                last = pe.transpose(p_uv[0:2 * R, c * P:(c + 1) * P], uv[:, c, :], ident)
            last.then_inc(uvt_ps, 1)
            pe.wait_ge(emb_set, 1)
            pe.wait_ge(ada_in, 16)
            for n in range(2 * B):
                b, half = divmod(n, 2)
                if n >= 2:
                    pe.wait_ge(ada_out, n - 1)
                for c in range(KC):
                    last = pe.matmul(p_ada[n % 2][:, :], emb[:, c, b:b + 1].to_broadcast([P, P]),
                                     wada[:, c, half * D:(half + 1) * D], start=c == 0, stop=c == KC - 1)
                last.then_inc(ada_ps, 1)
            pe.wait_ge(w1_in, 16)
            for c in range(KC):
                last = pe.transpose(p_w1[:, c * P:(c + 1) * P], w1[:, c * P:(c + 1) * P], ident)
            last.then_inc(w1t_ps, 1)
            pe.wait_ge(rw4_set, 4)
            for c in range(KC):
                last = pe.transpose(p_rw[:, c * P:(c + 1) * P], rw4[:, c, :], ident)
            last.then_inc(rw_ps, 1)
            pe.wait_ge(ones_set, 1)
            for b in range(B):
                pe.wait_ge(x_in[b % 2], 16 * (b // 2 + 1))
                if b >= 2:
                    pe.wait_ge(sum_set, b - 1)
                for t in range(NQT):
                    last = pe.matmul(p_sum[b % 2][0:1, :], ones[:, :], xin[:, b % 2, t, :], start=t == 0, stop=t == NQT - 1)
                last.then_inc(sum_ps, 1)
            pe.wait_ge(sum_set, B)
            for c in range(KC):
                for b in range(B):
                    last = pe.matmul(p_small[:, c * B + b:c * B + b + 1], sums[0:1, b, c * P:(c + 1) * P], ones[0:1, 0:1],
                                     start=True, stop=True)
            last.then_inc(pooled_ps, 1)
            pe.wait_ge(pooled_set, 1)
            pe.wait_ge(w1t_set, 1)
            for c in range(KC):
                last = pe.matmul(p_small[:, 32:32 + B], w1t[:, c, :], pooled[:, c * B:(c + 1) * B], start=c == 0, stop=c == KC - 1)
            last.then_inc(hid_ps, 1)
            pe.wait_ge(hid_set, 1)
            pe.wait_ge(gate_in, 64)
            pe.matmul(p_small[:, 64:64 + B], gw2[:, 0:1].to_broadcast([P, P]), hid[:, :], start=True, stop=True).then_inc(gate_ps, 1)
            pe.wait_ge(ortho, 1)
            for c in range(KC):
                last = pe.transpose(p_uv[:, c * 2 * R:(c + 1) * 2 * R], uvt[:, c * P:(c + 1) * P], keep["ident"][0:2 * R, 0:2 * R])
            last.then_inc(basis_ps, 1)
            pe.wait_ge(basis_set, 1)
            pe.wait_ge(ada_out, 2 * B)
            for c in range(KC):
                last = pe.matmul(p_ada[0][0:R, 0:R], basis[:, c, R:2 * R], basis[:, c, R:2 * R], start=c == 0, stop=c == KC - 1)
            last.then_inc(vtv_ps, 1)
            pe.wait_ge(vtv_set, 1)
            pe.matmul(p_ada[1][0:R, 0:R], vtv[:, :], uvt[0:R, 0:R], start=True, stop=True).then_inc(core_ps, 1)
            pe.wait_ge(core_set, 1)
            for c in range(KC):
                last = pe.matmul(p_uv[:, c * P:(c + 1) * P], uvt[0:R, c * P:(c + 1) * P], core4[:, :], start=True, stop=True)
            last.then_inc(m_ps, 1)

        @block.scalar
        def _(act):
            act.wait_ge(arg_set, 1)
            act.activation(turns[:, :, :], arg[:, :, :], ACT.Sin).then_inc(act_own, 1)
            act.wait_ge(act_own, 1)
            act.activation(emb[:, :, :], turns[:, :, :], ACT.Silu).then_inc(emb_set, 1)
            act.wait_ge(later_set, 2)
            for i in range(R):
                act.wait_ge(row_set, i + 1)
                act.activation(sq_junk[:, :], row[:, :], ACT.Square, accum_out=norm2[:, :]).then_inc(act_own, 1)
                act.wait_ge(act_own, i + 2)
                act.activation(norm[:, :], norm2[:, :], ACT.Sqrt).then_inc(norm_set, 1)
                act.wait_ge(dot_set, i + 1)
                act.activation(coef[:, 0:1], dot[:, 0:1], ACT.Copy, scale=later[:, i:i + 1]).then_inc(later_dot, 1)
                if 1 <= i <= 2 * B:
                    b, half = divmod(i - 1, 2)
                    act.wait_ge(ada_ps, i)
                    act.activation(cond[:, b, half * D:(half + 1) * D], p_ada[(i - 1) % 2][:, :], ACT.Copy).then_inc(ada_out, 1)
                if i == 10:
                    act.wait_ge(w1t_ps, 1)
                    act.activation(w1t[:, :, :], p_w1[:, :].rearrange("p (c n) -> p c n", c=KC), ACT.Copy).then_inc(w1t_set, 1)
                if i == 11:
                    act.wait_ge(rw_ps, 1)
                    act.activation(keep["rw"][:, :], p_rw[:, :], ACT.Copy).then_inc(rw_hi, 1)
                if i in (14, 18, 22, 26):
                    b = (i - 14) // 4
                    act.wait_ge(sum_ps, b + 1)
                    act.activation(sums[0:1, b, :], p_sum[b % 2][0:1, :], ACT.Copy).then_inc(sum_set, 1)
                if i == 28:
                    act.wait_ge(pooled_ps, 1)
                    act.activation(pooled[:, :], p_small[:, 0:KC * B], ACT.Copy).then_inc(pooled_set, 1)
                if i == 30:
                    act.wait_ge(hid_ps, 1)
                    act.wait_ge(gate_in, 64)
                    act.activation(hid[:, :], p_small[:, 32:32 + B], ACT.Relu, bias=gb1[:, :], scale=1.0 / S).then_inc(hid_set, 1)
            act.wait_ge(gate_ps, 1)
            act.activation(gate[:, 0, :], p_small[:, 64:64 + B], ACT.Sigmoid, bias=gb2[:, :]).then_inc(gate_set, 1)
            act.activation(gate[:, 1, :], safety[:, :], ACT.Sigmoid).then_inc(gate_set, 1)

        @block.vector
        def _(dve):
            link = chain_on(dve, dve_own)
            dve.wait_ge(tok_in, 16)
            dve.wait_ge(freq_in, 16)
            link(dve.tensor_copy(tokf[:, 0, :], tok[:, :]))
            link(dve.tensor_scalar(tokf[:, 1, :], tokf[:, 0, :], 0.01, 4000.0, ALU.mult, ALU.mult))
            for c in range(2):
                link(dve.tensor_scalar(angle[:, c, :], tokf[:, 1, :], freq[:, c:c + 1], None, ALU.mult))
            for q, quarter in enumerate((0.0, 0.25)):
                t, a = turns[:, 2 * q:2 * q + 2, :], arg[:, 2 * q:2 * q + 2, :]
                link(dve.tensor_scalar(t, angle[:, :, :], 1.0 / (2 * math.pi), quarter, ALU.mult, ALU.add))
                link(dve.tensor_scalar(t, t, ROUND, -ROUND, ALU.add, ALU.add))
                link(dve.scalar_tensor_tensor(a, t, -TWO_PI[0], angle[:, :, :], ALU.mult, ALU.add))
                link(dve.scalar_tensor_tensor(a, t, -TWO_PI[1], a, ALU.mult, ALU.add))
                link(dve.scalar_tensor_tensor(a, t, -TWO_PI[2], a, ALU.mult, ALU.add))
                link(dve.tensor_scalar(a, a, quarter * 2 * math.pi, PI_MAX, ALU.add, ALU.min))
                last = dve.tensor_scalar(a, a, -PI_MAX, None, ALU.max)
                if q == 0:
                    link(last)
            last.then_inc(arg_set, 1)

            dve.wait_ge(uvt_ps, 1)
            link(dve.tensor_copy(uvt[:, :], p_uv[0:2 * R, :]))
            dve.wait_ge(eye_set, 2)
            dve.wait_ge(later_set, 2)
            for i in range(R):
                dve.stream_shuffle(row[:, :], uvt[:, :], [i] * R).then_inc(row_set, 1)
                dve.wait_ge(row_set, i + 1)
                dve.tensor_tensor_reduce(dot_junk[:, :], row[:, :], uvt[:, :], 1.0, 0.0, ALU.mult, ALU.add, dot[:, :]).then_inc(dot_set, 1)
                dve.wait_ge(norm_set, i + 1)
                link(dve.tensor_scalar(normeps[:, :], norm[:, :], 1e-8, None, ALU.add))
                link(dve.reciprocal(inv[:, i:i + 1], normeps[:, :]))
                dve.wait_ge(later_dot, i + 1)
                link(dve.tensor_scalar(coef[:, 1:2], coef[:, 0:1], inv[:, i:i + 1], inv[:, i:i + 1], ALU.mult, ALU.mult))
                link(dve.scalar_tensor_tensor(uvt[:, :], row[:, :], coef[:, 1:2], uvt[:, :], ALU.mult, ALU.add))
            link(dve.tensor_tensor_reduce(dot_junk[:, 0:R], inv[:, :], eye[:, :], 1.0, 0.0, ALU.mult, ALU.add, own[:, :]))
            dve.tensor_scalar(uvt[:, :], uvt[:, :], own[:, 0:1], None, ALU.mult).then_inc(ortho, 1)
            dve.wait_ge(basis_ps, 1)
            dve.tensor_copy(basis[:, :, :], p_uv[:, 0:KC * 2 * R].rearrange("p (c r) -> p c r", c=KC)).then_inc(basis_set, 1)
            dve.wait_ge(vtv_ps, 1)
            dve.tensor_copy(vtv[:, :], p_ada[0][0:R, 0:R]).then_inc(vtv_set, 1)
            dve.wait_ge(core_ps, 1)
            dve.tensor_copy(core4[:, :].rearrange("p (q r) -> p q r", q=4),
                            p_ada[1][0:R, 0:R].unsqueeze(1).to_broadcast([R, 4, R])).then_inc(core_set, 1)
            dve.wait_ge(rw_hi, 1)
            for q in (1, 3):
                rows = slice(q * R, (q + 1) * R)
                link(dve.tensor_tensor(keep["rw"][rows, :], p_rw[rows, :], keep["rw"][rows, :].bitcast(F32), ALU.subtract))
            dve.wait_ge(m_ps, 1)
            link(dve.tensor_copy(keep["m4"][:, :, :], p_uv[:, :].rearrange("p (c n) -> p c n", c=KC)))


def projections(nc, io, keep, scratch):
    with ExitStack() as ctx:
        k = Scope(nc, ctx, "a_")
        x = k.sb("x", [P, NT, D])
        xt = k.sb("xt", [P, KC, TB])
        feat = k.sb("feat", [P, TB], F32R)
        y = k.sb("y", [P, NT, D])
        xo = k.sb("xo", [P, NT, D])
        stats = k.sb("stats", [P, NT, 6])
        meanvar = k.sb("meanvar", [P, NT, 2])
        rstd = k.sb("rstd", [P, NT, 2])
        xm_hi = k.sb("xm_hi", [P, KC, TB], F32R)
        xm_lo = k.sb("xm_lo", [P, KC, TB], F32R)
        out_f = k.sb("out_f", [P, RING, TB])
        out_hi = k.sb("out_hi", [P, RING, TB], F32R)
        out_lo = k.sb("out_lo", [P, RING, TB], F32R)
        v = k.sb("v", [P, 2, D])
        cond = k.sb("cond", [P, CW])
        bias_v = k.sb("bias_v", [P, D])
        bias_o = k.sb("bias_o", [P, D])
        bias_qk = k.sb("bias_qk", [P, 2, KC])
        mask8 = k.sb("mask8", [P, 2, S], U8)
        maskb = k.sb("maskb", [P, 2, S], BF16)

        p_out = [k.ps(f"p_out{i}", [P, 512]) for i in range(3)]
        p_t = [k.ps(f"p_t{i}", [P, 512]) for i in range(2)]
        p_feat = k.ps("p_feat", [P, 512])
        p_resp = [k.ps(f"p_resp{i}", [P, 512]) for i in range(2)]
        xm_bank = p_t + p_resp

        x_in, cond_in, bias_in = k.sem("x_in"), k.sem("cond_in"), k.sem("bias_in")
        mask_in, mask_out = k.sems("mask_in", 2), k.sems("mask_out", 2)
        qk_out, v_out, xo_out = k.sems("qk_out", RING), k.sems("v_out", 2), k.sem("xo_out")
        xt_ps, xt_set, feat_ps, feat_hi, feat_set, resp_ps = (k.sem(n) for n in ("xt_ps", "xt_set", "feat_ps", "feat_hi", "feat_set", "resp_ps"))
        xs_set, y_set, bn_set, stats_set, eps_set, rstd_set = (k.sem(n) for n in ("xs_set", "y_set", "bn_set", "stats_set", "eps_set", "rstd_set"))
        ln_set, scaled_set, xm_set, xo_set, xmt_ps, hi_set, lo_set = (
            k.sem(n) for n in ("ln_set", "scaled_set", "xm_set", "xo_set", "xmt_ps", "hi_set", "lo_set"))
        out_ps, qk_act, qk_lo, v_set, bq_set, mask_set = (k.sem(n) for n in ("out_ps", "qk_act", "qk_lo", "v_set", "bq_set", "mask_set"))
        ctx.callback(k.close)
        block = ctx.enter_context(nc.Block())

        NQK = 2 * KC
        NOUT = NQK + NT
        NMASK = B * NQT // NBLK
        scale = 1.0 / math.sqrt(HD)
        x_blk = io["x"].rearrange("b (n t p) d -> (b n) p t d", t=NT, p=P)
        xo_blk = scratch["xo"].rearrange("(n t p) d -> n p t d", t=NT, p=P)
        mask_blk = io["mask_Bx1xSxS_bk0"].rearrange("b o (t p) k -> (b o t) p k", p=P)
        parts = [scratch[n].rearrange("(m g) s r n -> m g s r n", g=KC) for n in ("q", "k")]
        v_blk = scratch["v"].rearrange("(m g) p t c -> m t p g c", g=KC)

        def slots(eng, prologue, slot):
            prologue(0)
            slot(0, False)
            with eng.Fori(1, NBLK - 1) as m:
                slot(m, False)
            slot(NBLK - 1, True)

        @block.sync
        def _(sp):
            def load(n):
                at_least(sp, y_set, NT * n)
                sp.dma_start(x[:, :, :], x_blk[n]).then_inc(x_in, 16)

            def load_cond(n, b):
                at_least(sp, xm_set, NT * n)
                sp.dma_start(cond[:, :], scratch["cond"][b].partition_broadcast(P)).then_inc(cond_in, 16)

            def store_xo(n):
                sp.wait_ge(xo_set, NT * (n + 1))
                sp.dma_start(xo_blk[n], xo[:, :, :]).then_inc(xo_out, 16)

            def slot(m, last):
                for i in range(NQK):
                    side, g = divmod(i, KC)
                    sp.wait_ge(qk_act, NQK * m + i + 1)
                    sp.dma_start(parts[side][m, g, 0], out_hi[:, i % RING, :].bitcast(F32)).then_inc(qk_out[i % RING], 16)
                    sp.wait_ge(qk_lo, NQK * m + i + 1)
                    sp.dma_start(parts[side][m, g, 1], out_lo[:, i % RING, :].bitcast(F32)).then_inc(qk_out[i % RING], 16)
                more = not last and not (isinstance(m, int) and m == NBLK - 2)
                if more:
                    load(m + 2)
                for t in range(NT):
                    sp.wait_ge(v_set, NT * m + t + 1)
                    sp.dma_start(v_blk[m, t], v[:, t % 2, :].rearrange("p (g c) -> p g c", g=KC)).then_inc(v_out[t % 2], 16)
                if more:
                    load_cond(m + 2, (m + 2) // 2)
                if not last:
                    store_xo(m + 1)

            load(0)
            load_cond(0, 0)
            sp.dma_start(bias_v[:, :], io["L1_cond_bv"].partition_broadcast(P)).then_inc(bias_in, 16)
            sp.dma_start(bias_o[:, :], io["L1_cond_bo"].partition_broadcast(P)).then_inc(bias_in, 16)
            sp.dma_start(bias_qk[:, 0, :], io["L1_cond_bq"].rearrange("(c p) -> p c", p=P)).then_inc(bias_in, 16)
            sp.dma_start(bias_qk[:, 1, :], io["L1_cond_bk"].rearrange("(c p) -> p c", p=P)).then_inc(bias_in, 16)
            load(1)
            load_cond(1, 0)
            store_xo(0)
            slot(0, False)
            with sp.Fori(1, NBLK - 2) as m:
                slot(m, False)
            slot(NBLK - 2, False)
            slot(NBLK - 1, True)
            for i in range(RING):
                sp.wait_ge(qk_out[i], 32 * NBLK * NQK // RING)
            for i in range(2):
                sp.wait_ge(v_out[i], 16 * NBLK * NT // 2)
            sp.wait_ge(xo_out, 16 * NBLK)

        @block.gpsimd
        def _(pool):
            def residual(n):
                pool.wait_ge(bias_in, 64)
                at_least(pool, xo_out, 16 * n)
                for t in range(NT):
                    pool.wait_ge(xm_set, NT * n + t + 1)
                    pool.tensor_tensor(xo[:, t, :], y[:, t, :], bias_o[:, :], ALU.add).then_inc(xo_set, 1)

            def front(n):
                pool.wait_ge(cond_in, 16 * (n + 1))
                pool.wait_ge(x_in, 16 * (n + 1))
                pool.wait_ge(xt_ps, KC * (n + 1))
                for t in range(NT):
                    pool.tensor_tensor(x[:, t, :], x[:, t, :], cond[:, 2 * D:3 * D], ALU.add).then_inc(xs_set, 1)
                for t in range(NT):
                    pool.wait_ge(stats_set, NT * n + t + 1)
                    pool.tensor_tensor(rstd[:, t, 0:1], meanvar[:, t, 1:2], keep["eps"][:, :], ALU.add).then_inc(eps_set, 1)
                    pool.wait_ge(eps_set, NT * n + t + 1)
                    pool.tensor_tensor(rstd[:, t, 1:2], rstd[:, t, 0:1], keep["neghalf"][:, :], ALU.pow).then_inc(rstd_set, 1)
                residual(n)

            front(0)
            front(1)
            with pool.Fori(1, NBLK - 1) as m:
                front(m + 1)

        @block.tensor
        def _(pe):
            ident = keep["ident"][:, :]

            def transpose_x(n, c):
                if c == 0:
                    pe.wait_ge(x_in, 16 * (n + 1))
                if c < 2:
                    at_least(pe, lo_set, KC * (n - 1) + c + 1)
                else:
                    pe.wait_ge(xt_set, KC * n + c - 1)
                for t in range(NT):
                    last = pe.transpose(p_t[c % 2][:, t * P:(t + 1) * P], x[:, t, c * P:(c + 1) * P], ident)
                last.then_inc(xt_ps, 1)

            def features(n):
                pe.wait_ge(xt_set, KC * (n + 1))
                at_least(pe, feat_set, n)
                for c in range(KC):
                    last = pe.matmul(p_feat[:, :], keep["m4"][:, c, :], xt[:, c, :], start=c == 0, stop=c == KC - 1)
                last.then_inc(feat_ps, 1)

            def response(n, t):
                pe.wait_ge(feat_set, n + 1)
                if t < 2:
                    at_least(pe, lo_set, KC * n - 1 + t)
                else:
                    pe.wait_ge(y_set, NT * n + t - 1)
                pe.matmul(p_resp[t % 2][:, :], feat[:, t * P:(t + 1) * P], keep["rw"][:, :], start=True, stop=True).then_inc(resp_ps, 1)

            def transpose_xm(n, c):
                if c == 0:
                    pe.wait_ge(xm_set, NT * (n + 1))
                if c < 2:
                    pe.wait_ge(xt_set, KC * n + 3 + c)
                for t in range(NT):
                    last = pe.transpose(xm_bank[c][:, t * P:(t + 1) * P], y[:, t, c * P:(c + 1) * P], ident)
                last.then_inc(xmt_ps, 1)

            def output(m, i):
                bank = i % 3
                before = i - 3
                if before >= NQK:
                    pe.wait_ge(v_set, NT * m + before - NQK + 1)
                elif before >= 0:
                    pe.wait_ge(qk_act, NQK * m + before + 1)
                else:
                    at_least(pe, v_set, NT * m + before + 1)
                out = p_out[bank][:, :]
                if i < NQK:
                    side, j = divmod(i, KC)
                    w_hi, w_lo = keep["wqkv"][side]
                    cols = slice(j * P, (j + 1) * P)
                    parts = [((w_hi[:, c, cols], xm_hi[:, c, :]), (w_lo[:, c, cols], xm_hi[:, c, :]), (w_hi[:, c, cols], xm_lo[:, c, :]))
                             for c in range(KC)]
                else:
                    w_hi, w_lo = keep["wqkv"][2]
                    cols = slice((i - NQK) * P, (i - NQK + 1) * P)
                    parts = [((xm_hi[:, c, cols], w_hi[:, c, :]), (xm_hi[:, c, cols], w_lo[:, c, :]), (xm_lo[:, c, cols], w_hi[:, c, :]))
                             for c in range(KC)]
                products = [(three[n], c) for c, three in enumerate(parts) for n in (0, 1)] + [(three[2], c) for c, three in enumerate(parts)]
                for n, ((left, right), c) in enumerate(products):
                    if i == 0 and n < 2 * KC and n % 2 == 0:
                        pe.wait_ge(hi_set, KC * m + c + 1)
                    if i == 0 and n >= 2 * KC:
                        pe.wait_ge(lo_set, KC * m + c + 1)
                    last = pe.matmul(out, left, right, start=n == 0, stop=n == len(products) - 1)
                last.then_inc(out_ps, 1)

            def front(n):
                for c in range(KC):
                    transpose_x(n, c)
                features(n)
                for t in range(NT):
                    response(n, t)
                for c in range(KC):
                    transpose_xm(n, c)

            def slot(m, last):
                for i in range(NOUT):
                    output(m, i)
                    if last:
                        continue
                    if i == 0:
                        for c in range(KC):
                            transpose_x(m + 1, c)
                    if i == 1:
                        features(m + 1)
                    if 2 <= i < 2 + NT:
                        response(m + 1, i - 2)
                    if i == NOUT - 2:
                        for c in range(KC):
                            transpose_xm(m + 1, c)

            slots(pe, front, slot)

        @block.scalar
        def _(act):
            def mask_tile(m, i):
                buf = i % 2
                act.wait_ge(mask_in[buf], 16 * (NMASK // 2 * m + i // 2 + 1))
                at_least(act, mask_out[buf], 16 * (NMASK // 2 * m + i // 2))
                act.activation(maskb[:, buf, :], mask8[:, buf, :], ACT.Copy, scale=MASKED).then_inc(mask_set, 1)
                act.wait_ge(mask_set, NMASK * m + i + 1)
                act.dma_start(scratch["mask"][NMASK * m + i], maskb[:, buf, :]).then_inc(mask_out[buf], 16)
                if not (isinstance(m, int) and m == NBLK - 1 and i >= NMASK - 2):
                    act.dma_start(mask8[:, buf, :], mask_blk[NMASK * m + i + 2]).then_inc(mask_in[buf], 16)

            for i in range(2):
                act.dma_start(mask8[:, i, :], mask_blk[i]).then_inc(mask_in[i], 16)

            def empty_xt(n, c):
                act.wait_ge(xt_ps, KC * n + c + 1)
                at_least(act, feat_ps, n)
                act.activation(xt[:, c, :], p_t[c % 2][:, :], ACT.Copy).then_inc(xt_set, 1)

            def high(n, c):
                act.wait_ge(xmt_ps, KC * n + c + 1)
                at_least(act, out_ps, NOUT * n)
                act.activation(xm_hi[:, c, :], xm_bank[c][:, :], ACT.Copy).then_inc(hi_set, 1)

            def front(n):
                for c in range(KC):
                    empty_xt(n, c)
                for c in range(KC):
                    high(n, c)
                act.wait_ge(bias_in, 64)
                act.activation(bias_qk[:, 0, :], bias_qk[:, 0, :], ACT.Copy, scale=scale).then_inc(bq_set, 1)
                act.wait_ge(bq_set, 1)

            def slot(m, last):
                for i in range(NOUT):
                    if i < NQK:
                        side, j = divmod(i, KC)
                        r = i % RING
                        act.wait_ge(out_ps, NOUT * m + i + 1)
                        at_least(act, qk_out[r], 32 * (NQK // RING * m + i // RING))
                        bias = bias_qk[:, side, j:j + 1]
                        act.activation(out_f[:, r, :], p_out[i % 3][:, :], ACT.Identity, bias=bias, scale=(scale, 1.0)[side])
                        act.activation(out_hi[:, r, :], p_out[i % 3][:, :], ACT.Identity, bias=bias, scale=(scale, 1.0)[side]).then_inc(qk_act, 1)
                    if i == 0 and not last:
                        for c in range(KC):
                            empty_xt(m + 1, c)
                    if 4 <= i < 4 + NMASK:
                        mask_tile(m, i - 4)
                if not last:
                    for c in range(KC):
                        high(m + 1, c)

            slots(act, front, slot)
            for buf in range(2):
                act.wait_ge(mask_out[buf], 16 * NBLK * NMASK // 2)

        @block.vector
        def _(dve):

            def cut_features(n):
                dve.wait_ge(feat_ps, n + 1)
                at_least(dve, resp_ps, NT * n)
                dve.tensor_copy(feat[:, :], p_feat[:, :]).then_inc(feat_hi, 1)
                dve.wait_ge(feat_hi, n + 1)
                low = slice(2 * R, 4 * R)
                dve.tensor_tensor(feat[low, :], p_feat[low, :], feat[low, :].bitcast(F32), ALU.subtract).then_inc(feat_set, 1)

            def condition(n, t):
                tile = NT * n + t + 1
                dve.wait_ge(resp_ps, tile)
                dve.wait_ge(xs_set, tile)
                if t == 0:
                    at_least(dve, xmt_ps, KC * n)
                    at_least(dve, xo_set, NT * n)
                dve.scalar_tensor_tensor(y[:, t, :], p_resp[t % 2][:, :], cond[:, 3 * D:3 * D + 1], x[:, t, :],
                                         ALU.mult, ALU.add).then_inc(y_set, 1)
                dve.wait_ge(y_set, tile)
                dve.bn_stats(stats[:, t, :], y[:, t, :]).then_inc(bn_set, 1)
                carried(dve, bn_set)
                dve.wait_ge(bn_set, tile)
                dve.bn_aggr(meanvar[:, t, :], stats[:, t, :]).then_inc(stats_set, 1)

            def modulate(n, t):
                tile = NT * n + t + 1
                dve.wait_ge(rstd_set, tile)
                dve.wait_ge(stats_set, tile)
                dve.tensor_scalar(y[:, t, :], y[:, t, :], meanvar[:, t, 0:1], rstd[:, t, 1:2], ALU.subtract, ALU.mult).then_inc(ln_set, 1)
                dve.wait_ge(ln_set, tile)
                dve.tensor_tensor(y[:, t, :], y[:, t, :], cond[:, 0:D], ALU.mult).then_inc(scaled_set, 1)
                dve.wait_ge(scaled_set, tile)
                dve.tensor_tensor(y[:, t, :], y[:, t, :], cond[:, D:2 * D], ALU.add).then_inc(xm_set, 1)

            def low(n, c):
                dve.wait_ge(hi_set, KC * n + c + 1)
                dve.tensor_tensor(xm_lo[:, c, :], xm_bank[c][:, :], xm_hi[:, c, :].bitcast(F32), ALU.subtract).then_inc(lo_set, 1)

            def front(n):
                cut_features(n)
                for t in range(NT):
                    condition(n, t)
                for t in range(NT):
                    modulate(n, t)
                for c in range(KC):
                    low(n, c)
                dve.wait_ge(bias_in, 64)

            def slot(m, last):
                for i in range(NOUT):
                    if i < NQK:
                        dve.wait_ge(qk_act, NQK * m + i + 1)
                        r = i % RING
                        dve.tensor_tensor(out_lo[:, r, :], out_f[:, r, :], out_hi[:, r, :].bitcast(F32), ALU.subtract).then_inc(qk_lo, 1)
                    else:
                        t = i - NQK
                        dve.wait_ge(out_ps, NOUT * m + i + 1)
                        at_least(dve, v_out[t % 2], 16 * (NT // 2 * m + t // 2))
                        dve.tensor_tensor(v[:, t % 2, :], p_out[i % 3][:, :], bias_v[:, :], ALU.add).then_inc(v_set, 1)
                    if last:
                        continue
                    if i == 1:
                        cut_features(m + 1)
                    if 2 <= i < 2 + NT:
                        condition(m + 1, i - 2)
                    if 4 <= i < 4 + NT:
                        modulate(m + 1, i - 4)
                if not last:
                    for c in range(KC):
                        low(m + 1, c)

            slots(dve, front, slot)


def attention(nc, io, keep, scratch):
    with ExitStack() as ctx:
        k = Scope(nc, ctx, "b_")
        q = k.sb("q", [P, 2, HG, QP], F32R)
        key = k.sb("key", [P, HG, S], F32R)
        val = k.sb("val", [P, NKC, P])
        bias = k.sb("bias", [P, NBIAS, S])
        mask = k.sb("mask", [P, NQT, S], BF16)
        prob = k.sb("prob", [P, NPROB, S])
        probt = k.sb("probt", [P, 2, HG, NKC, QP])
        negmax = k.sb("negmax", [P, 2, UQ])
        total = k.sb("total", [P, 2, UQ])
        recip = k.sb("recip", [P, 3, UQ])
        spread = k.sb("spread", [P, UQ, HD])
        recipt = k.sb("recipt", [P, QP])
        ctxn = k.sb("ctxn", [P, 2, QP])

        p_s = [k.ps(f"p_s{i}", [P, S]) for i in range(2)]
        p_ta, p_tb = k.ps("p_ta", [P, 512]), [k.ps(f"p_tb{i}", [P, 512]) for i in range(2)]
        p_pair = k.ps("p_pair", [P, 512])
        p_ctx, p_rec = p_pair[:, 0:QP], p_pair[:, QP:2 * QP]

        bias_in, q_in, key_in, mask_in = k.sems("bias_in", NBIAS), k.sems("q_in", 2), k.sems("key_in", HG), k.sems("mask_in", NQT)
        half_ps, tb_act = k.sem("half_ps"), k.sem("tb_act")
        val_in, ctx_out, key_set = k.sems("val_in", 2), k.sems("ctx_out", 2), k.sem("key_set")
        qk_ps, masked, score_set, prob_set, ta_ps, tb_ps, ta_set, tb_set = (
            k.sem(n) for n in ("qk_ps", "masked", "score_set", "prob_set", "ta_ps", "tb_ps", "ta_set", "tb_set"))
        recip_set, nan_set, spread_set, rec_ps, rec_set, ctx_ps, ctx_set = (
            k.sem(n) for n in ("recip_set", "nan_set", "spread_set", "rec_ps", "rec_set", "ctx_ps", "ctx_set"))
        ctx.callback(k.close)
        block = ctx.enter_context(nc.Block())

        VALUES_AT = ((0,), (1,), (2,), (3, 4), (5,), (6,), (7,), ())
        bias_u = io["fside_Bx16xSxS_0"].rearrange("b h (t p) k -> (b h) t p k", p=P)
        q_g = scratch["q"].rearrange("m s (h r) (u n) -> m s u r h n", h=HG, n=QP)
        key_g = scratch["k"].rearrange("(b f g) s (h r) n -> b g s h r f n", f=2, g=HG, h=HG)
        QUARTERS = [slice(s * HD, (s + 1) * HD) for s in range(4)]
        Q_PARTS, KEY_PARTS = (0, 0, 1, 1), (0, 1, 0, 1)
        FREE_AT = 5
        KEY_AT = UG - 6
        ctx_g = scratch["ctx"]

        def at_half(g, half):
            return g + HG * (g // HG) + HG * half

        def unit(j):
            return j // UQ, j % UQ // 2, j % 2

        def masked_before(j):
            return sum(i % UQ not in PE_MASKS for i in range(j))

        def second_halves(g, j, by_scalar):
            def counts(i):
                return (i % UQ in ACT_BOTH) == by_scalar

            inside = sum(map(counts, range(j))) - sum(map(counts, range(j, 0)))
            return NQP * (len(ACT_BOTH) if by_scalar else UQ - len(ACT_BOTH)) * g + inside

        def groups(eng, group):
            group(0, True, False)
            with eng.Fori(1, NG - 1) as g:
                group(g, False, False)
            group(NG - 1, False, True)

        def ahead(g, j, last):
            if j < UG:
                return g, j
            return None if last else (g + 1, j - UG)

        @block.sync
        def _(sp):
            def load_q(g, u):
                at_least(sp, qk_ps, UG * g + UQ * (u - 1))
                for rows, part in zip(QUARTERS, Q_PARTS):
                    sp.dma_start(q[rows, u % 2, :, :].bitcast(F32), q_g[at_half(g, u // 2), part, u % 2]).then_inc(q_in[u % 2], 16)

            def load_key(b, i, h):
                at_least(sp, qk_ps, UG * (HG * b + i - 1) + UG - UQ + 2 * h + 2)
                for rows, part in zip(QUARTERS[:2], KEY_PARTS):
                    sp.dma_start(key[rows, h, :].rearrange("r (f n) -> r f n", f=2).bitcast(F32),
                                 key_g[b, i, part, h]).then_inc(key_in[h], 16)

            def load_mask(b, i, u):
                for tile in range(2 * u, 2 * u + 2):
                    at_least(sp, score_set, UG * (HG * b + i - 1) + UQ * (u + 1))
                    sp.dma_start(mask[:, tile, :], scratch["mask"][NQT * b + tile]).then_inc(mask_in[tile], 16)

            def group(b, i, masks):
                g = HG * b + i
                very_first = isinstance(g, int) and g == 0
                for j in range(UG):
                    u, h, t = unit(j)
                    if j % UQ == (0 if very_first and u == 0 else FREE_AT):
                        load_q(g, u)
                        if masks and j:
                            load_mask(b, i, u)
                    at = j if very_first else j - FREE_AT
                    if at in range(0, UQ, 2):
                        load_key(b, i, at // 2)
                    at_least(sp, prob_set, UG * g + j - NBIAS + 1)
                    sp.dma_start(bias[:, j % NBIAS, :], bias_u[HG * g + h, 2 * u + t]).then_inc(bias_in[j % NBIAS], 16)
                    if very_first and j == 0:
                        load_mask(b, i, u)

            group(0, 0, True)
            with sp.Fori(1, HG) as i:
                group(0, i, False)
            with sp.Fori(1, B) as b:
                group(b, 0, True)
                with sp.Fori(1, HG) as i:
                    group(b, i, False)

        @block.gpsimd
        def _(pool):
            def group(g, first, last):
                for j in range(UG):
                    u, h, t = unit(j)
                    if j % UQ in PE_MASKS:
                        continue
                    if j % UQ == 0:
                        pool.wait_ge(mask_in[2 * u], 16 * (g // HG + 1))
                        pool.wait_ge(mask_in[2 * u + 1], 16 * (g // HG + 1))
                    buf = j % NBIAS
                    pool.wait_ge(bias_in[buf], 16 * (UG // NBIAS * g + j // NBIAS + 1))
                    pool.tensor_tensor(bias[:, buf, :], bias[:, buf, :], mask[:, 2 * u + t, :], ALU.add).then_inc(masked, 1)

            with pool.Fori(0, NG) as g:
                group(g, False, False)

        @block.tensor
        def _(pe):
            def scores(g, j):
                u, h, t = unit(j)
                at_least(pe, score_set, UG * g + j - 1)
                if j % UQ == 0:
                    pe.wait_ge(q_in[u % 2], 64 * (NQP // 2 * g + u // 2 + 1))
                if j < UQ and t == 0:
                    pe.wait_ge(key_set, HG * g + h + 1)
                on_pe = j % UQ in PE_MASKS
                if on_pe:
                    pe.wait_ge(mask_in[2 * u + t], 16 * (g // HG + 1))
                for n in range(S // 512):
                    cols = slice(n * 512, (n + 1) * 512)
                    last = pe.matmul(p_s[j % 2][:, cols], q[:, u % 2, h, t * P:(t + 1) * P], key[:, h, cols], start=True, stop=not on_pe)
                    if on_pe:
                        last = pe.matmul(p_s[j % 2][:, cols], keep["identb"][:, :], mask[:, 2 * u + t, cols], start=False, stop=True)
                last.then_inc(qk_ps, 1)

            def transposes(g, j, half):
                unit_no = UG * g + j
                if half == 0:
                    bank, made = p_ta, ta_ps
                    pe.wait_ge(prob_set, unit_no + 1)
                    at_least(pe, ta_set, unit_no)
                else:
                    bank, made = p_tb[j % 2], tb_ps
                    if (j - 2) % UQ in ACT_BOTH:
                        at_least(pe, tb_act, second_halves(g, j - 1, True))
                    else:
                        at_least(pe, tb_set, second_halves(g, j - 1, False))
                for c in range(NKC // 2):
                    kc = half * (NKC // 2) + c
                    last = pe.transpose(bank[:, c * P:(c + 1) * P], prob[:, j % NPROB, kc * P:(kc + 1) * P], keep["ident"][:, :])
                last.then_inc(made, 1)

            def values(g, u, kc):
                if kc == 0:
                    pairs = NQP * g + u
                    pe.wait_ge(ta_set, UQ * (pairs + 1))
                    pe.wait_ge(tb_set, (UQ - len(ACT_BOTH)) * (pairs + 1))
                    if ACT_BOTH:
                        pe.wait_ge(tb_act, len(ACT_BOTH) * (pairs + 1))
                    at_least(pe, ctx_set, pairs)
                if kc % (NKC // 2) == 0:
                    pe.wait_ge(val_in[kc // (NKC // 2)], 16 * (g + 1))
                for h in range(HG):
                    rows = slice(h * HD, (h + 1) * HD)
                    last = pe.matmul(p_ctx[rows, :], val[:, kc, rows], probt[:, u % 2, h, kc, :], start=kc == 0, stop=kc == NKC - 1)
                if kc == NKC // 2 - 1:
                    last.then_inc(half_ps, 1)
                if kc == NKC - 1:
                    last.then_inc(ctx_ps, 1)

            def reciprocals(g, u):
                pairs = NQP * g + u
                pe.wait_ge(spread_set, pairs + 1)
                at_least(pe, ctx_set, pairs)
                for t in range(2):
                    last = pe.transpose(p_rec[:, t * P:(t + 1) * P], spread[:, t * HG:(t + 1) * HG, :].rearrange("p h d -> p (h d)"),
                                        keep["ident"][:, :])
                last.then_inc(rec_ps, 1)

            def group(g, first, last):
                for j in range(UG):
                    u, r = j // UQ, j % UQ
                    then = ahead(g, j + SCORES_AHEAD, last)
                    if then:
                        scores(*then)
                    of = None if first and u == 0 else (g, u - 1) if u else (g - 1, NQP - 1)
                    chunks = VALUES_AT[r] if of else ()
                    transposes(g, j, 0)
                    if r:
                        for kc in chunks[:1]:
                            values(*of, kc)
                    transposes(g, j, 1)
                    for kc in chunks[1:] if r else chunks:
                        values(*of, kc)
                    if of and r == UQ - 1:
                        reciprocals(*of)

            for j in range(SCORES_AHEAD):
                scores(0, j)
            groups(pe, group)
            for kc in range(NKC):
                values(NG - 1, NQP - 1, kc)
            reciprocals(NG - 1, NQP - 1)

        @block.scalar
        def _(act):
            def exponentials(g, j):
                u, h, t = unit(j)
                s = UG * g + j
                act.wait_ge(score_set, s + 1)
                at_least(act, tb_ps, s - NPROB + 1)
                if j % UQ == 0:
                    at_least(act, spread_set, NQP * g + u - 1)
                col = t * HG + h
                act.activation(prob[:, j % NPROB, :], bias[:, j % NBIAS, :], ACT.Exp, bias=negmax[:, u % 2, col:col + 1], scale=-1.0,
                               accum_out=total[:, u % 2, col:col + 1]).then_inc(prob_set, 1)

            def half_a(g, j):
                u, h, t = unit(j)
                act.wait_ge(ta_ps, UG * g + j + 1)
                if j % UQ == 0:
                    at_least(act, ctx_ps, NQP * g + u - 1)
                act.activation(probt[:, u % 2, h, 0:NKC // 2, t * P:(t + 1) * P], p_ta[:, :].rearrange("p (c n) -> p c n", n=P),
                               ACT.Copy).then_inc(ta_set, 1)
                if j % UQ in ACT_BOTH:
                    act.wait_ge(tb_ps, UG * g + j + 1)
                    act.activation(probt[:, u % 2, h, NKC // 2:NKC, t * P:(t + 1) * P], p_tb[j % 2][:, :].rearrange("p (c n) -> p c n", n=P),
                                   ACT.Copy).then_inc(tb_act, 1)

            def reciprocals(g, u):
                pairs = NQP * g + u
                act.wait_ge(rec_ps, pairs + 1)
                at_least(act, ctx_set, pairs)
                act.activation(recipt[:, :], p_rec, ACT.Copy).then_inc(rec_set, 1)

            def store(g, u):
                act.wait_ge(ctx_set, NQP * g + u + 1)
                act.dma_start(ctx_g[at_half(g, u // 2), :, (u % 2) * QP:(u % 2 + 1) * QP],
                              ctxn[:, u % 2, :]).then_inc(ctx_out[u % 2], 16)

            def load_values(g, half):
                at_least(act, (half_ps, ctx_ps)[half], NQP * g)
                act.dma_start(val[:, half * NT:(half + 1) * NT, :], scratch["v"][at_half(g, half)]).then_inc(val_in[half], 16)

            def group(g, first, last):
                for j in range(UG):
                    u, r = j // UQ, j % UQ
                    then = ahead(g, j + EXP_AHEAD, last)
                    if then:
                        exponentials(*then)
                    half_a(g, j)
                    if j in (4, UQ - 1) and not first:
                        load_values(g, j // 5)
                    if first and u == 0:
                        continue
                    of = (g, u - 1) if u else (g - 1, NQP - 1)
                    if r == 0 and (u > 1 or not first):
                        before = (g, u - 2) if u > 1 else (g - 1, NQP - 2 + u)
                        store(*before)
                    if r == UQ - 1:
                        reciprocals(*of)

            load_values(0, 0)
            load_values(0, 1)
            for j in range(EXP_AHEAD):
                exponentials(0, j)
            groups(act, group)
            store(NG - 1, NQP - 2)
            reciprocals(NG - 1, NQP - 1)
            store(NG - 1, NQP - 1)
            for i in range(2):
                act.wait_ge(ctx_out[i], 16 * NG * NQP // 2)

        @block.vector
        def _(dve):
            def biased(g, j):
                u, h, t = unit(j)
                s = UG * g + j
                if j % UQ not in PE_MASKS:
                    addend, there = masked, counted(dve, masked_before(UG) * g + masked_before(j) + 1)
                else:
                    addend, there = bias_in[j % NBIAS], counted(dve, 16 * (UG // NBIAS * g + j // NBIAS + 1))
                scored = counted(dve, s + 1)
                before = counted(dve, s - 2 * UQ + UQ)
                carried(dve, qk_ps)
                dve.wait_ge(qk_ps, scored)
                dve.wait_ge(addend, there)
                if j % UQ == 0:
                    at_least(dve, prob_set, before)
                col = t * HG + h
                dve.tensor_tensor_reduce(bias[:, j % NBIAS, :], p_s[j % 2][:, :], bias[:, j % NBIAS, :], -1.0, HUGE,
                                         ALU.add, ALU.min, negmax[:, u % 2, col:col + 1]).then_inc(score_set, 1)

            def half_b(g, j):
                u, h, t = unit(j)
                dve.wait_ge(tb_ps, UG * g + j + 1)
                if j % UQ == 0:
                    at_least(dve, ctx_ps, NQP * g + u - 1)
                dve.tensor_copy(probt[:, u % 2, h, NKC // 2:NKC, t * P:(t + 1) * P],
                                p_tb[j % 2][:, :].rearrange("p (c n) -> p c n", n=P)).then_inc(tb_set, 1)

            def reciprocals(g, u):
                pairs = NQP * g + u
                dve.wait_ge(prob_set, UQ * (pairs + 1))
                dve.reciprocal(recip[:, 0, :], total[:, u % 2, :]).then_inc(recip_set, 1)
                dve.tensor_scalar(recip[:, 1, :], negmax[:, u % 2, :], -0.1 * MASKED, HUGE, ALU.is_gt, ALU.mult).then_inc(nan_set, 1)
                dve.wait_ge(nan_set, 2 * pairs + 1)
                dve.tensor_scalar(recip[:, 2, :], recip[:, 1, :], HUGE, 0.0, ALU.mult, ALU.mult).then_inc(nan_set, 1)
                dve.wait_ge(nan_set, 2 * pairs + 2)
                dve.wait_ge(recip_set, pairs + 1)
                at_least(dve, rec_ps, pairs)
                dve.tensor_tensor(spread[:, :, :], recip[:, 0, :].unsqueeze(2).to_broadcast([P, UQ, HD]),
                                  recip[:, 2, :].unsqueeze(2).to_broadcast([P, UQ, HD]), ALU.add).then_inc(spread_set, 1)

            def normalize(g, u):
                pairs = NQP * g + u
                dve.wait_ge(ctx_ps, pairs + 1)
                dve.wait_ge(rec_set, pairs + 1)
                at_least(dve, ctx_out[u % 2], 16 * (NQP // 2 * g + u // 2))
                dve.tensor_tensor(ctxn[:, u % 2, :], p_ctx, recipt[:, :], ALU.mult).then_inc(ctx_set, 1)

            def spread_key(g, h):
                dve.wait_ge(key_in[h], 32 * (g + 1))
                dve.tensor_copy(key[P // 2:P, h, :], key[0:P // 2, h, :].bitcast(F32)).then_inc(key_set, 1)

            def group(g, first, last):
                for j in range(UG):
                    u, r = j // UQ, j % UQ
                    then = ahead(g, j + BIASED_AHEAD, last)
                    if then:
                        biased(*then)
                    if j in (KEY_AT, KEY_AT + 2, KEY_AT + 4) and not last:
                        spread_key(g + 1, (j - KEY_AT) // 2)
                    if first and j in (0, 2):
                        spread_key(g, HG // 2 + j // 2)
                    if j == KEY_AT + 6 - UG and not first:
                        spread_key(g, HG - 1)
                    if j % UQ not in ACT_BOTH:
                        half_b(g, j)
                    if first and u == 0:
                        continue
                    of = (g, u - 1) if u else (g - 1, NQP - 1)
                    if r == 1:
                        reciprocals(*of)
                    if r == UQ - 1:
                        normalize(*of)

            for j in range(BIASED_AHEAD):
                if j % 2 == 0:
                    spread_key(0, j // 2)
                biased(0, j)
            groups(dve, group)
            reciprocals(NG - 1, NQP - 1)
            normalize(NG - 1, NQP - 1)


def feed_forward(nc, io, keep, scratch, out):
    with ExitStack() as ctx:
        k = Scope(nc, ctx, "f_")
        wo = [k.sb(f"wo{i}", [P, KC, D], F32R) for i in range(2)]
        w1 = [k.sb(f"w1{i}", [P, KC, FF], F32R) for i in range(2)]
        w2 = [k.sb(f"w2{i}", [P, FC, D], F32R) for i in range(2)]
        cx = k.sb("cx", [P, KC, P])
        cx_hi = k.sb("cx_hi", [P, 2, KC, P], F32R)
        cx_lo = k.sb("cx_lo", [P, 2, KC, P], F32R)
        y = k.sb("y", [P, NT, D])
        yb = k.sb("yb", [P, D])
        stats = k.sb("stats", [P, NT, 6])
        meanvar = k.sb("meanvar", [P, NT, 2])
        rstd = k.sb("rstd", [P, NT, 2])
        ht_f = k.sb("ht_f", [P, 2, TB])
        ht_hi = k.sb("ht_hi", [P, KC, TB], F32R)
        ht_lo = k.sb("ht_lo", [P, KC, TB], F32R)
        act_f = k.sb("act_f", [P, 2, TB])
        act_hi = k.sb("act_hi", [P, 2, TB], F32R)
        act_lo = k.sb("act_lo", [P, 2, TB], F32R)
        o = k.sb("o", [P, NT, D])
        g2 = k.sb("g2", [P, KC])
        beta2 = k.sb("beta2", [P, KC])
        b1 = k.sb("b1", [P, 2, FC])
        b2 = k.sb("b2", [P, D])

        p_h = [k.ps(f"p_h{i}", [P, 512]) for i in range(2)]
        p_o = [k.ps(f"p_o{i}", [P, 512]) for i in range(NT)]
        p_f = [k.ps(f"p_f{i}", [P, 512]) for i in range(2)]
        t_bank = p_f + p_h

        w_in, small_in, cx_in, y_in, yb_out, yb_in, o_out = (
            k.sems("w_in", NT), k.sem("small_in"), k.sem("cx_in"), k.sem("y_in"), k.sem("yb_out"), k.sems("yb_in", NT), k.sems("o_out", NT))
        w_hi, w_lo, b1_set, cx_hi_set, cx_set, proj_ps, y_set, bn_set, stats_set, eps_set, rstd_set = (
            k.sem(n) for n in ("w_hi", "w_lo", "b1_set", "cx_hi_set", "cx_set", "proj_ps", "y_set", "bn_set", "stats_set", "eps_set", "rstd_set"))
        yb_set, ln_set, t_ps, htf_set, hi_set, lo_set, up_ps, sig_set, act_set, act_hi_set, act_lo_set, down_ps, out_ps, o_set = (
            k.sem(n) for n in ("yb_set", "ln_set", "t_ps", "htf_set", "hi_set", "lo_set", "up_ps", "sig_set", "act_set", "act_hi_set",
                               "act_lo_set", "down_ps", "out_ps", "o_set"))
        ctx.callback(k.close)
        block = ctx.enter_context(nc.Block())

        wo_v = io["L1_cond_Wo"].rearrange("(c p) n -> c p n", p=P)
        w1_v = io["L1_cond_W1"].rearrange("(c p) (g n) -> g c p n", p=P, n=D)
        w2_v = io["L1_cond_W2"].rearrange("(f p) n -> f p n", p=P)
        pieces = [(wo_v[c], wo, (c, slice(0, D))) for c in range(KC)]
        pieces += [(w1_v[0, c], w1, (c, slice(0, D))) for c in range(KC)]
        FIRST = len(pieces)
        due = []
        for f in range(FC):
            pieces.append((w2_v[f], w2, (f, slice(0, D))))
            g = f // KC + 1
            if g < FF // D:
                pieces.append((w1_v[g, f % KC], w1, (f % KC, slice(g * D, (g + 1) * D))))
            due.append(len(pieces))

        def due_w1(f):
            return FIRST if f < KC else due[KC * (f // KC) - 1]

        xo_blk = scratch["xo"].rearrange("(n t p) d -> n p t d", t=NT, p=P)
        yb_blk = scratch["yb"].rearrange("(n t p) d -> n t p d", t=NT, p=P)
        out_blk = out.rearrange("b (n t p) d -> (b n) t p d", t=NT, p=P)
        ctx_blk = scratch["ctx"].rearrange("(n c) p (t q) -> n t p c q", c=KC, t=NT)

        def slots(eng, front, slot):
            front(0)
            slot(0, False)
            with eng.Fori(1, NBLK - 1) as m:
                slot(m, False)
            slot(NBLK - 1, True)

        @block.sync
        def _(sp):
            def load_y(n):
                at_least(sp, t_ps, KC * n)
                sp.dma_start(y[:, :, :], xo_blk[n]).then_inc(y_in, 16)

            def load_cx(n, t):
                at_least(sp, cx_set, NT * n + t)
                sp.dma_start(cx[:, :, :], ctx_blk[n, t]).then_inc(cx_in, 16)

            def store_yb(n, t):
                sp.wait_ge(yb_set, NT * n + t + 1)
                sp.dma_start(yb_blk[n, t], yb[:, :]).then_inc(yb_out, 16)

            def load_yb(m, t):
                written, free = counted(sp, 16 * (NT * m + t + 1)), counted(sp, 16 * m)
                sp.wait_ge(yb_out, written)
                at_least(sp, o_out[t], free)
                sp.dma_start(o[:, t, :], yb_blk[m, t]).then_inc(yb_in[t], 16)

            def store_o(m, t):
                sp.wait_ge(o_set, NT * m + t + 1)
                sp.dma_start(out_blk[m, t], o[:, t, :]).then_inc(o_out[t], 16)

            def front(n):
                load_y(n)
                for t in range(NT):
                    load_cx(n, t)
                    if t >= 2:
                        store_yb(n, t - 2)
                for t in range(NT - 2, NT):
                    store_yb(n, t)

            def outputs(m):
                for t in range(NT):
                    load_yb(m, t)
                for t in range(NT):
                    store_o(m, t)

            def load_pieces(first, end):
                for n in range(first, end):
                    at_least(sp, w_lo, n - NT + 1)
                    sp.dma_start(o[:, n % NT, :], pieces[n][0]).then_inc(w_in[n % NT], 16)

            load_pieces(0, KC)
            load_cx(0, 0)
            load_y(0)
            sp.dma_start(b1[:, 0, :], io["L1_cond_b1"].rearrange("(f p) -> p f", p=P)).then_inc(small_in, 16)
            sp.dma_start(g2[:, :], io["L1_cond_g2"].rearrange("(c p) -> p c", p=P)).then_inc(small_in, 16)
            sp.dma_start(beta2[:, :], io["L1_cond_beta2"].rearrange("(c p) -> p c", p=P)).then_inc(small_in, 16)
            sp.dma_start(b2[:, :], io["L1_cond_b2"].partition_broadcast(P)).then_inc(small_in, 16)
            for t in range(1, NT):
                load_cx(0, t)
                load_pieces(KC + t - 1, KC + t)
                if t >= 2:
                    store_yb(0, t - 2)
            for t in range(NT - 2, NT):
                store_yb(0, t)
            load_pieces(FIRST - 1, FIRST)
            for f in range(FC):
                load_pieces(due[f - 1] if f else FIRST, due[f])
                if f == 0:
                    load_y(1)
                if f in (0, 2, 4, 6):
                    load_cx(1, f // 2)
                if f in (4, 6, 8, 10):
                    store_yb(1, f // 2 - 2)
            sp.wait_ge(w_lo, len(pieces))
            outputs(0)
            with sp.Fori(1, NBLK - 1) as m:
                front(m + 1)
                outputs(m)
            outputs(NBLK - 1)
            for t in range(NT):
                sp.wait_ge(o_out[t], 16 * NBLK)

        @block.gpsimd
        def _(pool):
            pool.wait_ge(small_in, 64)

            def front(n):
                for t in range(NT):
                    tile = NT * n + t + 1
                    pool.wait_ge(y_set, tile)
                    at_least(pool, yb_out, 16 * (tile - 1))
                    pool.tensor_tensor(yb[:, :], y[:, t, :], b2[:, :], ALU.add).then_inc(yb_set, 1)
                    pool.wait_ge(stats_set, tile)
                    pool.tensor_tensor(rstd[:, t, 0:1], meanvar[:, t, 1:2], keep["eps"][:, :], ALU.add).then_inc(eps_set, 1)
                    pool.wait_ge(eps_set, tile)
                    pool.tensor_tensor(rstd[:, t, 1:2], rstd[:, t, 0:1], keep["neghalf"][:, :], ALU.pow).then_inc(rstd_set, 1)

            front(0)
            with pool.Fori(1, NBLK) as n:
                front(n)

        @block.tensor
        def _(pe):
            def project(n, t):
                if t == 0:
                    at_least(pe, w_lo, KC) if isinstance(n, int) else None
                pe.wait_ge(cx_set, NT * n + t + 1)
                if t < 2:
                    at_least(pe, lo_set, KC * n - 1 + t)
                else:
                    pe.wait_ge(y_set, NT * n + t - 1)
                products = []
                for c in range(KC):
                    hi, lo = cx_hi[:, t % 2, c, :], cx_lo[:, t % 2, c, :]
                    products += [(hi, wo[0][:, c, :]), (hi, wo[1][:, c, :]), (lo, wo[0][:, c, :])]
                for i, (left, right) in enumerate(products):
                    last = pe.matmul(p_f[t % 2][:, :], left, right, start=i == 0, stop=i == len(products) - 1)
                last.then_inc(proj_ps, 1)

            def transpose(n, c):
                if c == 0:
                    pe.wait_ge(ln_set, NT * (n + 1))
                if c >= 2:
                    at_least(pe, act_set, FC * n - 2 + c - 1)
                for t in range(NT):
                    last = pe.transpose(t_bank[c][:, t * P:(t + 1) * P], y[:, t, c * P:(c + 1) * P], keep["ident"][:, :])
                last.then_inc(t_ps, 1)

            def up(m, f):
                at_least(pe, act_set, FC * m + f - 1)
                if f == 0:
                    pe.wait_ge(lo_set, KC * m + 3)
                cols = slice(f * P, (f + 1) * P)
                if isinstance(m, int) and m == 0:
                    pe.wait_ge(w_lo, due_w1(f))
                products = [(w1[part][:, c, cols], ht_hi[:, c, :]) for c in range(KC) for part in range(2)]
                products += [(w1[0][:, c, cols], ht_lo[:, c, :]) for c in range(KC)]
                for i, (left, right) in enumerate(products):
                    if f == 0 and i == 2 * (KC - 1):
                        pe.wait_ge(hi_set, KC * (m + 1))
                    if f == 0 and i == 3 * KC - 1:
                        pe.wait_ge(lo_set, KC * (m + 1))
                    last = pe.matmul(p_h[f % 2][:, :], left, right, start=i == 0, stop=i == len(products) - 1)
                last.then_inc(up_ps, 1)

            def down(m, f):
                pe.wait_ge(act_lo_set, FC * m + f + 1)
                pe.wait_ge(act_hi_set, FC * m + f + 1)
                if isinstance(m, int) and m == 0:
                    pe.wait_ge(w_lo, due[f])
                for t in range(NT):
                    if f == 0:
                        at_least(pe, o_set, NT * (m - 1) + t + 1)
                    cols = slice(t * P, (t + 1) * P)
                    hi, lo = act_hi[:, f % 2, cols], act_lo[:, f % 2, cols]
                    pe.matmul(p_o[t][:, :], hi, w2[0][:, f, :], start=f == 0, stop=False)
                    pe.matmul(p_o[t][:, :], hi, w2[1][:, f, :], start=False, stop=False)
                    last = pe.matmul(p_o[t][:, :], lo, w2[0][:, f, :], start=False, stop=f == FC - 1)
                    if f == FC - 1:
                        last.then_inc(out_ps, 1)
                if f < FC - 1:
                    last.then_inc(down_ps, 1)

            def front(n):
                for t in range(NT):
                    project(n, t)
                for c in range(KC):
                    transpose(n, c)

            def slot(m, last):
                up(m, 0)
                up(m, 1)
                for f in range(FC):
                    if f + 2 < FC:
                        up(m, f + 2)
                    down(m, f)
                    if last:
                        continue
                    if f in (1, 3, 5, 7):
                        project(m + 1, (f - 1) // 2)
                    if f == FC - 4:
                        transpose(m + 1, 0)
                        transpose(m + 1, 1)
                    if f == FC - 2:
                        transpose(m + 1, 2)
                        transpose(m + 1, 3)

            slots(pe, front, slot)

        @block.scalar
        def _(act):
            def cut(first, end):
                for n in range(first, end):
                    _, w, at = pieces[n]
                    act.wait_ge(w_in[n % NT], 16 * (n // NT + 1))
                    act.activation(w[0][:, at[0], at[1]], o[:, n % NT, :], ACT.Copy).then_inc(w_hi, 1)

            def high_cx(n, t):
                tile = NT * n + t
                act.wait_ge(cx_in, 16 * (tile + 1))
                at_least(act, proj_ps, tile - 1)
                act.activation(cx_hi[:, t % 2, :, :], cx[:, :, :], ACT.Copy).then_inc(cx_hi_set, 1)

            def normed(n, c):
                act.wait_ge(t_ps, KC * n + c + 1)
                at_least(act, up_ps, FC * n)
                at_least(act, lo_set, KC * n + c - 1)
                act.activation(ht_f[:, c % 2, :], t_bank[c][:, :], ACT.Identity, scale=g2[:, c:c + 1], bias=beta2[:, c:c + 1]).then_inc(htf_set, 1)
                act.activation(ht_hi[:, c, :], t_bank[c][:, :], ACT.Identity, scale=g2[:, c:c + 1], bias=beta2[:, c:c + 1]).then_inc(hi_set, 1)

            def front(n):
                cut(0, KC)
                for t in range(NT):
                    high_cx(n, t)
                cut(KC, FIRST)
                act.wait_ge(small_in, 64)
                act.activation(b1[:, 1, :], b1[:, 0, :], ACT.Copy, scale=1.702).then_inc(b1_set, 1)
                act.wait_ge(b1_set, 1)
                for c in range(KC):
                    normed(n, c)

            def slot(m, last):
                for f in range(FC):
                    if isinstance(m, int) and m == 0:
                        cut(due[f - 1] if f else FIRST, due[f])
                    i = FC * m + f
                    act.wait_ge(up_ps, i + 1)
                    at_least(act, act_lo_set, i - 1)
                    at_least(act, act_hi_set, i - 1)
                    act.activation(act_f[:, f % 2, :], p_h[f % 2][:, :], ACT.Sigmoid, scale=1.702, bias=b1[:, 1, f:f + 1]).then_inc(sig_set, 1)
                    if last:
                        continue
                    if f in (0, 2, 4, 6):
                        high_cx(m + 1, f // 2)
                    if f == FC - 1:
                        for c in range(KC):
                            normed(m + 1, c)

            slots(act, front, slot)

        @block.vector
        def _(dve):
            def cut(first, end):
                for n in range(first, end):
                    dve.wait_ge(w_hi, n + 1)
                    _, w, at = pieces[n]
                    dve.tensor_tensor(w[1][:, at[0], at[1]], o[:, n % NT, :], w[0][:, at[0], at[1]].bitcast(F32), ALU.subtract).then_inc(w_lo, 1)

            def low_cx(n, t):
                dve.wait_ge(cx_hi_set, NT * n + t + 1)
                dve.tensor_tensor(cx_lo[:, t % 2, :, :], cx[:, :, :], cx_hi[:, t % 2, :, :].bitcast(F32), ALU.subtract).then_inc(cx_set, 1)

            def attended(n, t):
                tile = NT * n + t + 1
                dve.wait_ge(proj_ps, tile)
                dve.wait_ge(y_in, 16 * (n + 1))
                dve.tensor_tensor(y[:, t, :], p_f[t % 2][:, :], y[:, t, :], ALU.add).then_inc(y_set, 1)
                dve.wait_ge(y_set, tile)
                dve.bn_stats(stats[:, t, :], y[:, t, :]).then_inc(bn_set, 1)
                carried(dve, bn_set)
                dve.wait_ge(bn_set, tile)
                dve.bn_aggr(meanvar[:, t, :], stats[:, t, :]).then_inc(stats_set, 1)

            def normalize(n, t):
                tile = NT * n + t + 1
                dve.wait_ge(rstd_set, tile)
                dve.wait_ge(stats_set, tile)
                dve.wait_ge(yb_set, tile)
                dve.tensor_scalar(y[:, t, :], y[:, t, :], meanvar[:, t, 0:1], rstd[:, t, 1:2], ALU.subtract, ALU.mult).then_inc(ln_set, 1)

            def low(n, c):
                dve.wait_ge(hi_set, KC * n + c + 1)
                dve.wait_ge(htf_set, KC * n + c + 1)
                dve.tensor_tensor(ht_lo[:, c, :], ht_f[:, c % 2, :], ht_hi[:, c, :].bitcast(F32), ALU.subtract).then_inc(lo_set, 1)

            def front(n):
                cut(0, KC)
                for t in range(NT):
                    low_cx(n, t)
                    if t:
                        attended(n, t - 1)
                attended(n, NT - 1)
                for t in range(NT):
                    normalize(n, t)
                cut(KC, FIRST)
                dve.wait_ge(small_in, 64)
                for c in range(KC):
                    low(n, c)

            def slot(m, last):
                for f in range(FC):
                    if isinstance(m, int) and m == 0:
                        cut(due[f - 1] if f else FIRST, due[f])
                    i = FC * m + f
                    b = f % 2
                    dve.wait_ge(sig_set, i + 1)
                    dve.scalar_tensor_tensor(act_f[:, b, :], p_h[b][:, :], b1[:, 0, f:f + 1], act_f[:, b, :], ALU.add, ALU.mult).then_inc(act_set, 1)
                    dve.wait_ge(act_set, i + 1)
                    if f < 2:
                        at_least(dve, out_ps, NT * m)
                        at_least(dve, down_ps, (FC - 1) * m)
                    else:
                        dve.wait_ge(down_ps, (FC - 1) * m + f - 1)
                    dve.tensor_copy(act_hi[:, b, :], act_f[:, b, :]).then_inc(act_hi_set, 1)
                    dve.wait_ge(act_hi_set, i + 1)
                    dve.tensor_tensor(act_lo[:, b, :], act_f[:, b, :], act_hi[:, b, :].bitcast(F32), ALU.subtract).then_inc(act_lo_set, 1)
                    if not last:
                        if f in (0, 2, 4, 6):
                            low_cx(m + 1, f // 2)
                        if f in (2, 4, 6, 8):
                            attended(m + 1, f // 2 - 1)
                        if f == 10:
                            for t in range(NT):
                                normalize(m + 1, t)
                        if f == FC - 1:
                            for c in range(KC):
                                low(m + 1, c)
                for t in range(NT):
                    dve.wait_ge(out_ps, NT * m + t + 1)
                    dve.wait_ge(yb_in[t], 16 * (m + 1))
                    dve.tensor_tensor(o[:, t, :], p_o[t][:, :], o[:, t, :], ALU.add).then_inc(o_set, 1)

            slots(dve, front, slot)


def build(nc, io, out):
    with nc.allow_non_contiguous_dma(reason="bias columns of a few hundred elements"):
        build_stages(nc, io, out)


def build_stages(nc, io, out):
    scratch = {
        "cond": nc.dram_tensor("cond_scratch", (B, CW), F32).ap(),
        "q": nc.dram_tensor("q_scratch", (NBLK * KC, 2, P, TB), F32).ap(),
        "k": nc.dram_tensor("k_scratch", (NBLK * KC, 2, P, TB), F32).ap(),
        "v": nc.dram_tensor("v_scratch", (NBLK * KC, P, NT, P), F32).ap(),
        "mask": nc.dram_tensor("mask_scratch", (B * NQT, P, S), BF16).ap(),
        "xo": nc.dram_tensor("xo_scratch", (B * S, D), F32).ap(),
        "ctx": nc.dram_tensor("ctx_scratch", (NBLK * KC, P, TB), F32).ap(),
        "yb": nc.dram_tensor("yb_scratch", (B * S, D), F32).ap(),
    }
    with ExitStack() as ctx:
        k = Scope(nc, ctx, "k_")
        keep = {"ident": k.sb("ident", [P, P]), "identb": k.sb("identb", [P, P], BF16), "neghalf": k.sb("neghalf", [P, 1]), "eps": k.sb("eps", [P, 1])}
        with ExitStack() as early:
            e = Scope(nc, early, "e_")
            keep["m4"] = e.sb("m4", [P, KC, P])
            keep["rw"] = e.sb("rw", [P, D], F32R)
            keep["wqkv"] = [tuple(e.sb(f"w{n}{part}", [P, KC, D], F32R) for part in ("hi", "lo")) for n in "qkv"]
            conditioning(nc, io, keep, scratch)
            projections(nc, io, keep, scratch)
        attention(nc, io, keep, scratch)
        feed_forward(nc, io, keep, scratch, out)


def frequencies():
    half = D // 2
    freqs = np.exp(np.arange(half, dtype=np.float32) * np.float32(-math.log(10000.0) / (half - 1)))
    return np.ascontiguousarray(freqs.astype(np.float32).reshape(2, P).T)


def kernel(**inputs):
    import concourse.bacc as bacc
    from concourse.bass_utils import run_bass_kernel_spmd

    nc = bacc.Bacc("TRN2", target_bir_lowering=False, num_devices=1)
    arrays, io = {}, {}
    for name, value in [*inputs.items(), ("freq", frequencies())]:
        a = np.ascontiguousarray(value)
        arrays[f"in_{name}"] = a
        io[name] = nc.dram_tensor(f"in_{name}", a.shape, mybir.dt.from_np(a.dtype), kind="ExternalInput").ap()
    out = nc.dram_tensor("out", (B, S, D), F32, kind="ExternalOutput").ap()
    build(nc, io, out)
    result = run_bass_kernel_spmd(nc, [arrays], core_ids=[0])
    return result.results[0]["out"]
```
